# Optimizing a Trainium2 kernel written in Bass

```python
import numpy as np
import jax
import jax.numpy as jnp

def _softmax(x, axis=-1):
    return jax.nn.softmax(x, axis=axis)

def _gelu(x):
    return jax.nn.gelu(x, approximate=True)

def _silu(x):
    return jax.nn.silu(x)

def _sigmoid(x):
    return jax.nn.sigmoid(x)

def _layernorm(x, axis=-1, eps=1e-05):
    m = jnp.mean(x, axis=axis, keepdims=True)
    v = jnp.var(x, axis=axis, keepdims=True)
    return (x - m) / jnp.sqrt(v + eps)

def _scatter_add(tgt, idx, src, axis=0):
    return tgt.at[idx].add(src)

def _segment_sum(src, seg, n):
    return jax.ops.segment_sum(src, seg, n)
kernel_name = 'mk_decoder_postln_d1_seqx_r8_7f6b75'

def setup_inputs(seed: int=0):
    np.random.seed(seed)
    _w = jnp.asarray

    def _rec_inputs():
        import jax
        import jax.numpy as jnp
        _rk = jax.random.key(seed)
        x = 0.002226 + 0.9996 * jax.random.normal(jax.random.fold_in(_rk, 1), (4, 256, 128), jnp.float32)
        _lenS = 256 - jax.random.randint(jax.random.fold_in(_rk, 7), (4,), 0, max(1, 256 // 4) + 1, jnp.int32)
        _lenS2 = 256 - jax.random.randint(jax.random.fold_in(_rk, 8), (4,), 0, max(1, 256 // 4) + 1, jnp.int32)
        _ctx_1024P = jax.random.normal(jax.random.fold_in(_rk, 11), (4, 16, 128), jnp.float32)
        _ctx_1024c = jax.random.dirichlet(jax.random.fold_in(_rk, 511), 0.3 * jnp.ones((16,), jnp.float32), (4, 256))
        _ctx_1024t = jnp.einsum('bsk,bkd->bsd', _ctx_1024c, _ctx_1024P)
        _ctx_1024t = _ctx_1024t * jax.lax.rsqrt(jnp.mean(jnp.square(_ctx_1024t)) + 1e-12) * 0.953939
        ctx_1024 = -0.000125008 + 0.999885 * (_ctx_1024t + 0.3 * jax.random.normal(jax.random.fold_in(_rk, 611), (4, 256, 128), jnp.float32))
        return (x, ctx_1024)
    x, ctx_1024 = _rec_inputs()

    def _L0_attn_setup():
        import jax, jax.numpy as jnp
        import numpy as np
        B, S, D = (4, 128, 128)
        H, M = (16, 64)
        HD = D // H
        key = jax.random.key(seed)
        ks = jax.random.split(key, 8)
        return {'query': jax.random.normal(ks[0], (B, S, D), dtype=jnp.float32), 'w_qkv': jax.random.normal(ks[1], (3 * D, D), dtype=jnp.float32) * D ** (-0.5), 'b_qkv': jax.random.normal(ks[2], (3 * D,), dtype=jnp.float32) * 0.02, 'w_out': jax.random.normal(ks[3], (D, D), dtype=jnp.float32) * D ** (-0.5), 'b_out': jax.random.normal(ks[4], (D,), dtype=jnp.float32) * 0.02, 'freq_q': jax.random.normal(ks[5], (H, M, HD), dtype=jnp.float32), 'freq_k': jax.random.normal(ks[6], (H, M, HD), dtype=jnp.float32), 'freq_v': jax.random.normal(ks[7], (H, M, HD), dtype=jnp.float32)}
    _L0_attn_all = _L0_attn_setup()
    _L0_attn_in = {k: v for k, v in _L0_attn_all.items() if k in ('w_qkv', 'b_qkv', 'w_out', 'b_out', 'freq_q', 'freq_k', 'freq_v')}
    del _L0_attn_all

    def _L0_xattn_setup():
        import jax, jax.numpy as jnp
        import numpy as np
        EPS = 1e-05

        def layer_norm(x, g, b):
            mu = jnp.mean(x, axis=-1, keepdims=True)
            var = jnp.var(x, axis=-1, keepdims=True)
            return (x - mu) * jax.lax.rsqrt(var + EPS) * g + b
        key = jax.random.key(seed)
        ks = jax.random.split(key, 8)
        dim, heads, dim_head = (128, 16, 64)
        inner = heads * dim_head
        b, n, m = (8, 512, 64)
        s = dim ** (-0.5)
        return {'x': jax.random.normal(ks[0], (b, n, dim), jnp.float32), 'latents': jax.random.normal(ks[1], (b, m, dim), jnp.float32), 'ln_m_g': jnp.ones((dim,), jnp.float32), 'ln_m_b': jnp.zeros((dim,), jnp.float32), 'ln_l_g': jnp.ones((dim,), jnp.float32), 'ln_l_b': jnp.zeros((dim,), jnp.float32), 'Wq': jax.random.normal(ks[2], (dim, inner), jnp.float32) * s, 'Wkv': jax.random.normal(ks[3], (dim, 2 * inner), jnp.float32) * s, 'Wout': jax.random.normal(ks[4], (inner, dim), jnp.float32) * s}
    _L0_xattn_all = _L0_xattn_setup()
    _L0_xattn_in = {k: v for k, v in _L0_xattn_all.items() if k in ('ln_m_g', 'ln_m_b', 'ln_l_g', 'ln_l_b', 'Wq', 'Wkv', 'Wout')}
    del _L0_xattn_all

    def _L0_ffn_setup():
        import jax, jax.numpy as jnp
        import numpy as np
        TOP_K = 2
        key = jax.random.key(seed)
        k0, k1, k2, k3, k4 = jax.random.split(key, 5)
        B, S, D, H, E = (4, 256, 128, 256, 8)
        x = jax.random.normal(k0, (B, S, D), dtype=jnp.float32)
        router_w = jax.random.normal(k1, (E, D), dtype=jnp.float32) * D ** (-0.5)
        w_gate = jax.random.normal(k2, (E, D, H), dtype=jnp.float32) * D ** (-0.5)
        w_up = jax.random.normal(k3, (E, D, H), dtype=jnp.float32) * D ** (-0.5)
        w_down = jax.random.normal(k4, (E, H, D), dtype=jnp.float32) * H ** (-0.5)
        return {'x': x, 'router_w': router_w, 'w_gate': w_gate, 'w_up': w_up, 'w_down': w_down}
    _L0_ffn_all = _L0_ffn_setup()
    _L0_ffn_in = {k: v for k, v in _L0_ffn_all.items() if k in ('router_w', 'w_gate', 'w_up', 'w_down')}
    del _L0_ffn_all
    return {'x': x, 'ctx_1024': ctx_1024, 'L0_attn_w_qkv': _L0_attn_in['w_qkv'], 'L0_attn_b_qkv': _L0_attn_in['b_qkv'], 'L0_attn_w_out': _L0_attn_in['w_out'], 'L0_attn_b_out': _L0_attn_in['b_out'], 'L0_attn_freq_q': _L0_attn_in['freq_q'], 'L0_attn_freq_k': _L0_attn_in['freq_k'], 'L0_attn_freq_v': _L0_attn_in['freq_v'], 'L0_xattn_ln_m_g': _L0_xattn_in['ln_m_g'], 'L0_xattn_ln_m_b': _L0_xattn_in['ln_m_b'], 'L0_xattn_ln_l_g': _L0_xattn_in['ln_l_g'], 'L0_xattn_ln_l_b': _L0_xattn_in['ln_l_b'], 'L0_xattn_Wq': _L0_xattn_in['Wq'], 'L0_xattn_Wkv': _L0_xattn_in['Wkv'], 'L0_xattn_Wout': _L0_xattn_in['Wout'], 'L0_ffn_router_w': _L0_ffn_in['router_w'], 'L0_ffn_w_gate': _L0_ffn_in['w_gate'], 'L0_ffn_w_up': _L0_ffn_in['w_up'], 'L0_ffn_w_down': _L0_ffn_in['w_down']}

def reference(x, ctx_1024, L0_attn_w_qkv, L0_attn_b_qkv, L0_attn_w_out, L0_attn_b_out, L0_attn_freq_q, L0_attn_freq_k, L0_attn_freq_v, L0_xattn_ln_m_g, L0_xattn_ln_m_b, L0_xattn_ln_l_g, L0_xattn_ln_l_b, L0_xattn_Wq, L0_xattn_Wkv, L0_xattn_Wout, L0_ffn_router_w, L0_ffn_w_gate, L0_ffn_w_up, L0_ffn_w_down):
    import jax
    import jax.numpy as jnp

    def _L0_attn_ref(query, w_qkv, b_qkv, w_out, b_out, freq_q, freq_k, freq_v):
        import jax, jax.numpy as jnp
        import numpy as np
        B, S, D = (4, 128, 128)
        H, M = (16, 64)
        HD = D // H
        b, s, d = query.shape
        h, m, hd = freq_q.shape
        fft_base = jnp.fft.fft(jnp.eye(s, dtype=jnp.float32)).astype(jnp.complex64)
        qkv = query @ w_qkv.T + b_qkv
        q, k, v = jnp.split(qkv, 3, axis=-1)

        def heads(x):
            return x.reshape(b, s, h, hd).transpose(0, 2, 1, 3)
        q, k, v = (heads(q), heads(k), heads(v))

        def to_freq(x):
            xc = x.astype(jnp.complex64)
            return jnp.einsum('bhsd,fs->bhfd', xc, jnp.conj(fft_base))

        def filt(xf, w):
            xt = xf[:, :, :m] * w.astype(jnp.complex64)[None]
            return jnp.pad(xt, ((0, 0), (0, 0), (0, s - m), (0, 0)))
        q_fft = filt(to_freq(q), freq_q)
        k_fft = filt(to_freq(k), freq_k)
        v_fft = filt(to_freq(v), freq_v)
        scores = jnp.sum(jnp.real(q_fft * jnp.conj(k_fft)), axis=-1, keepdims=True)
        attn = jax.nn.softmax(scores, axis=2)
        out_fft = attn.astype(jnp.complex64) * v_fft
        out = jnp.real(jnp.einsum('bhfd,fs->bhsd', out_fft, fft_base))
        out = out.transpose(0, 2, 1, 3).reshape(b, s, d)
        return out @ w_out.T + b_out

    def _L0_xattn_ref(x, latents, ln_m_g, ln_m_b, ln_l_g, ln_l_b, Wq, Wkv, Wout):
        import jax, jax.numpy as jnp
        import numpy as np
        EPS = 1e-05

        def layer_norm(x, g, b):
            mu = jnp.mean(x, axis=-1, keepdims=True)
            var = jnp.var(x, axis=-1, keepdims=True)
            return (x - mu) * jax.lax.rsqrt(var + EPS) * g + b
        heads, dim_head = (16, 64)
        scale = dim_head ** (-0.5)
        x = layer_norm(x, ln_m_g, ln_m_b)
        lat = layer_norm(latents, ln_l_g, ln_l_b)
        b, m, _ = lat.shape
        q = lat @ Wq
        kv_input = jnp.concatenate([x, lat], axis=1)
        kv = kv_input @ Wkv
        k, v = jnp.split(kv, 2, axis=-1)

        def split_heads(t):
            return t.reshape(t.shape[0], t.shape[1], heads, dim_head).transpose(0, 2, 1, 3)
        q, k, v = (split_heads(q), split_heads(k), split_heads(v))
        dots = jnp.einsum('bhid,bhjd->bhij', q, k) * scale
        attn = jax.nn.softmax(dots, axis=-1)
        out = jnp.einsum('bhij,bhjd->bhid', attn, v)
        out = out.transpose(0, 2, 1, 3).reshape(b, m, heads * dim_head)
        return out @ Wout

    def _L0_ffn_ref(x, router_w, w_gate, w_up, w_down):
        import jax, jax.numpy as jnp
        import numpy as np
        TOP_K = 2
        B, S, D = x.shape
        E = router_w.shape[0]
        xt = x.reshape(-1, D)
        logits = xt @ router_w.T
        topk_vals, topk_idx = jax.lax.top_k(logits, TOP_K)
        g = jax.nn.sigmoid(topk_vals)
        g = g / (g.sum(axis=-1, keepdims=True) + 1e-10)
        out = jnp.zeros_like(xt)
        for e in range(E):
            ge = jnp.sum(jnp.where(topk_idx == e, g, jnp.zeros_like(g)), axis=-1)
            h = jax.nn.silu(xt @ w_gate[e]) * (xt @ w_up[e])
            out = out + ge[:, None] * (h @ w_down[e])
        return out.reshape(B, S, D)
    x = _layernorm(x + _L0_attn_ref(x, L0_attn_w_qkv, L0_attn_b_qkv, L0_attn_w_out, L0_attn_b_out, L0_attn_freq_q, L0_attn_freq_k, L0_attn_freq_v), axis=-1)
    x = _layernorm(x + _L0_xattn_ref(ctx_1024, x, L0_xattn_ln_m_g, L0_xattn_ln_m_b, L0_xattn_ln_l_g, L0_xattn_ln_l_b, L0_xattn_Wq, L0_xattn_Wkv, L0_xattn_Wout), axis=-1)
    x = _layernorm(x + _L0_ffn_ref(x, L0_ffn_router_w, L0_ffn_w_gate, L0_ffn_w_up, L0_ffn_w_down), axis=-1)
    return x

_drawn_inputs = setup_inputs


def setup_inputs(seed=0):
    import zlib

    import numpy as np

    out = dict(_drawn_inputs(seed))
    spreads = {'L0_xattn_ln_m_g': (1.0, 0.2),
     'L0_xattn_ln_m_b': (0.0, 0.1),
     'L0_xattn_ln_l_g': (1.0, 0.2),
     'L0_xattn_ln_l_b': (0.0, 0.1)}
    factors = {'L0_attn_b_out': 2.933}
    for name, (base, spread) in spreads.items():
        noise = np.random.default_rng([zlib.crc32(name.encode()), seed]).standard_normal(out[name].shape)
        drawn = base * np.exp(spread * noise) if base else spread * noise
        out[name] = jnp.asarray(drawn.astype(out[name].dtype))
    for name, factor in factors.items():
        out[name] = (out[name] * factor).astype(out[name].dtype)
    return out
```

```python
from contextlib import ExitStack

import concourse.bass as bass
from concourse import mybir

F32 = mybir.dt.float32
F32R = mybir.dt.float32r
F16 = mybir.dt.float16
U32 = mybir.dt.uint32
ALU = mybir.AluOpType
ACT = mybir.ActivationFunctionType
AX_X = mybir.AxisListType.X

P = 128
D = 128
B = 4
S = 256
C = S // P
M = 64
FH = 16
HD = D // FH
H = 16
DH = 64
J = 2 * S
JT = J // P
NH = B * H
E = 8
F = 256
FC = F // P
EPS = 1e-5
SCALE = DH ** -0.5
P_SCALE = 1024.0
V_SCALE = 64.0

CS0, CST0, ID0, EB0, SEL0, IO0, HALF0, LEN0, NCONST = 0, 256, 512, 640, 752, 1264, 1328, 1336, 1340


def decoder_layer(nc, x, ctx_in, w_qkvT, b_qkv, w_outT, b_out, freqT, ln_par, wqT, wkT, wv, wout,
                  routerT, w_gu, w_down, consts, out):
    with ExitStack() as ctx:
        def sb(name, shape, dt=F32):
            return ctx.enter_context(nc.sbuf_tensor(name, shape, dt))

        def sem(name):
            return ctx.enter_context(nc.semaphore(name))

        cst = sb("cst", [P, NCONST])
        xt = sb("xt", [P, C, B, D])
        ct = sb("ct", [P, C, B, D])
        x1 = sb("x1", [P, C, B, D])
        zl = sb("zl", [P, C, B, D])
        x2 = zl
        acc = xt
        wqkv_sb = sb("wqkv_sb", [P, 3 * D])
        bqkv_sb = sb("bqkv_sb", [1, 3 * D])
        wo_sb = sb("wo_sb", [P, D])
        bo_sb = sb("bo_sb", [1, D])
        fr_sb = sb("fr_sb", [P, 3, M])
        ln_sb = sb("ln_sb", [P, 4])
        wqk_sb = sb("wqk_sb", [P, 2, H // 2, D])
        wqT_sb, wkT_sb = wqk_sb[:, 0], wqk_sb[:, 1]
        wv_sb = sb("wv_sb", [P, H * DH])
        wvh = sb("wvh", [P, H * DH], F32R)
        wvl = sb("wvl", [P, H * DH], F32R)
        wo2 = sb("wo2", [P, H, D])
        rt_sb = sb("rt_sb", [P, E])
        work = sb("work", [P, 6, 512])
        ft = work[:, 0]
        fqk = sb("fqk", [P, M])
        qw = work[:, 1].rearrange("p (k m) -> p k m", m=M)
        qk = work[:, 2].rearrange("p (k m) -> p k m", m=M)
        vw = work[:, 3].rearrange("p (b a m) -> p b a m", b=B, a=2)
        ot = work[:, 4].rearrange("p (b a m) -> p b a m", b=B, a=2)
        fnmax = sb("fnmax", [B * FH, 1])
        fexp = sb("fexp", [B * FH, M])
        fsum = sb("fsum", [B * FH, 1])
        frcp = sb("frcp", [B * FH, 1])
        fattn = sb("fattn", [B * FH, M])
        g_sb = work[:, 5]
        st = sb("st", [P, 5, C * B, 6])
        mv = sb("mv", [P, 5, C * B, 2])
        ve = sb("ve", [P, 5, C * B])
        rs = sb("rs", [P, 5, C * B])
        ah = sb("ah", [P, H, D], F32R)
        al = sb("al", [P, H, D], F32R)
        kv = sb("kv", [P, B, J])
        kvh = sb("kvh", [P, B, J], F32R)
        kvl = sb("kvl", [P, B, J], F32R)
        th = sb("th", [P, 4, S], F32R)
        tl = sb("tl", [P, 4, S], F32R)
        vt = sb("vt", [P, 2, JT, H, 2 * DH], F16)
        pr = wqk_sb[:].rearrange("p a k d -> p (a k d)").rearrange("p (i j) -> p i j", i=4)
        nmax = sb("nmax", [P, 2 * NH])
        psm = sb("psm", [P, 2 * NH])
        rcp = sb("rcp", [P, 2 * NH])
        pth = sb("pth", [P, 2, C, JT, P], F16)
        ptl = sb("ptl", [P, 2, C, JT, P], F16)
        oT = sb("oT", [P, 3, S])
        wraw = ct[:].rearrange("p c b d -> p c (b d)")
        wgh = sb("wgh", [P, E, 2 * F], F32R)
        wgl = sb("wgl", [P, E, 2 * F], F32R)
        wd = kv[:].rearrange("p b j -> p (b j)").rearrange("p (e k n) -> p e k n", e=E, k=FC)
        xT = wv_sb[:].rearrange("p (b s) -> p b s", b=B)
        xTh = sb("xTh", [P, B, S], F32R)
        xTl = sb("xTl", [P, B, S], F32R)
        lg = sb("lg", [P, 8, E])
        top = sb("top", [P, 8, 8])
        topi = sb("topi", [P, 8, 8], U32)
        topf = sb("topf", [P, 8, 8])
        ge2 = sb("ge2", [P, 8, 2])
        gs = sb("gs", [P, 8])
        gr = sb("gr", [P, 8])
        gn = sb("gn", [P, 8, 2])
        m0 = sb("m0", [P, 8, E])
        m1 = sb("m1", [P, 8, E])
        gate = sb("gate", [P, 8, E])
        sg = work[:, 0:2]
        hT = work[:, 2:6].rearrange("p (i k) t -> p i k t", k=FC)

        bank = ctx.enter_context(nc.psum_tensor("bank", [P, 8, 512], F32))
        S_B, T_B, O_B, TB_B, V_B, Y_B = 0, 2, 4, 5, 6, 7

        LAT_B = (7, 1, 2, 3)
        ident = cst[:, ID0:ID0 + P]

        (d_x, d_cs, d_cst, d_ctx, d_wqkv, d_bq, d_fr, d_small, d_wq, d_wk, d_wv, d_wo2, d_rt,
         d_wd, d_out) = [sem(n) for n in (
            "d_x", "d_cs", "d_cst", "d_ctx", "d_wqkv", "d_bq", "d_fr", "d_small", "d_wq", "d_wk",
            "d_wv", "d_wo2", "d_rt", "d_wd", "d_out")]
        d_raw = [sem("d_raw0"), sem("d_raw1")]
        ft_made, ft_sb, qkv_made, fqk_made, qk_sb, vw_sb, fs_made, fnmax_made, fexp_made = [
            sem(n) for n in ("ft_made", "ft_sb", "qkv_made", "fqk_made", "qk_sb", "vw_sb",
                             "fs_made", "fnmax_made", "fexp_made")]
        fattn_sb, fab_made, ot_sb, g_made, g_copied, y1_made, a_made, ah_made, al_made = [
            sem(n) for n in ("fattn_sb", "fab_made", "ot_sb", "g_made", "g_copied", "y1_made",
                             "a_made", "ah_made", "al_made")]
        zc_made, ctxT_made, kv_made, kvh_made, kvl_made, zl_made, latT_made = [
            sem(n) for n in ("zc_made", "ctxT_made", "kv_made", "kvh_made", "kvl_made", "zl_made",
                             "latT_made")]
        wvh_made, wvl_made, v_made, vh_made, vl_made, t_made, th_made, tl_made = [
            sem(n) for n in ("wvh_made", "wvl_made", "v_made", "vh_made", "vl_made", "t_made",
                             "th_made", "tl_made")]
        s_made, max_made, exp_made, rcp_made, pn_made, pT_made, pth_made, ptl_made = [
            sem(n) for n in ("s_made", "max_made", "exp_made", "rcp_made", "pn_made", "pT_made",
                             "pth_made", "ptl_made")]
        o_made, o_sb, y_part, y_used, x2_made, x2T_made, xT_made, xTh_made, xTl_made = [
            sem(n) for n in ("o_made", "o_sb", "y_part", "y_used", "x2_made", "x2T_made",
                             "xT_made", "xTh_made", "xTl_made")]
        ve_made, rs_made, wgh_made, wgl_made = [
            sem(n) for n in ("ve_made", "rs_made", "wgh_made", "wgl_made")]
        lg_made, lg_copied, top_made, ge_made, gate_made = [
            sem(n) for n in ("lg_made", "lg_copied", "top_made", "ge_made", "gate_made")]
        gu_made, sg_made, h_made, dn_made, dn_used, fin_made = [
            sem(n) for n in ("gu_made", "sg_made", "h_made", "dn_made", "dn_used", "fin_made")]
        dve_own = sem("dve_own")

        STEPS = NH + 3

        def fold_slot(h):
            return 4 * (2 * (h // 8) + h % 2) + h % 8 // 2

        def v_group(n):
            if n % 2 == 0 or n >= NH - H:
                return None
            k = (n % H) // 2
            return n // H + 1, k // 2, k % 2

        def v_index(n):
            return 8 + min(n, NH - H) // 2

        def x2_step(b):
            return H * (b + 1) + 3

        def ffn_tail(b):
            return x2_step(b) + 3

        block = ctx.enter_context(nc.Block())

        @block.sync
        def _(sp):
            for c in range(C):
                sp.dma_start(xt[:, c], x.rearrange("b (c p) d -> c p b d", p=P)[c]).then_inc(d_x, 16)
            sp.dma_start(wqkv_sb[:], w_qkvT).then_inc(d_wqkv, 16)
            sp.dma_start(bqkv_sb[:], b_qkv).then_inc(d_bq, 16)
            sp.dma_start(fr_sb[:], freqT.rearrange("p (a m) -> p a m", a=3)).then_inc(d_fr, 16)
            sp.dma_start(wqT_sb, wqT.rearrange("(k p) d -> p k d", p=P)).then_inc(d_wq, 16)
            sp.dma_start(wkT_sb, wkT.rearrange("(k p) d -> p k d", p=P)).then_inc(d_wk, 16)
            sp.dma_start(wo_sb[:], w_outT).then_inc(d_small, 16)
            sp.dma_start(bo_sb[:], b_out).then_inc(d_small, 16)
            sp.dma_start(wv_sb[:], wv).then_inc(d_wv, 16)
            for r in range(2):
                sp.dma_start(wo2[r * DH:(r + 1) * DH], wout.rearrange("(h q) n -> q h n", q=DH)
                             ).then_inc(d_wo2, 16)
            sp.dma_start(rt_sb[:], routerT).then_inc(d_rt, 16)
            sp.wait_ge(ctxT_made, 2)
            for e in range(E):
                if e == 2:
                    sp.wait_ge(kvl_made, C + B)
                    sp.wait_ge(kvh_made, C + B)
                    sp.dma_start(wd, w_down.rearrange("e (c p) n -> p e c n", p=P)).then_inc(d_wd, 16)
                if e >= 2:
                    sp.wait_ge(wgl_made, e - 1)
                sp.dma_start(wraw[:, e % 2], w_gu[:, e]).then_inc(d_raw[e % 2], 16)
            for hf in range(2):
                sp.wait_ge(fin_made, 4 * (hf + 1))
                for c in range(C):
                    sp.dma_start(out.rearrange("b (c p) d -> c p b d", p=P)[c, :, 2 * hf:2 * hf + 2],
                                 acc[:, c, 2 * hf:2 * hf + 2]).then_inc(d_out, 16)
            sp.wait_ge(d_out, 16 * 2 * C)

        @block.tensor
        def _(pe):
            mm = nc.tensor.matmul

            def three(dst, wh, wl, mh, ml):
                mm(dst, wh, mh, start=True, stop=False)
                mm(dst, wh, ml, start=False, stop=False)
                return mm(dst, wl, mh, start=False, stop=True)

            pe.wait_ge(d_x, 32)
            pe.wait_ge(d_cs, 16)
            for b in range(B):
                for c in range(C):
                    last = mm(bank[:, 0, b * P:(b + 1) * P], xt[:, c, b],
                              cst[:, CS0 + c * P:CS0 + (c + 1) * P], start=(c == 0), stop=(c == C - 1))
            last.then_inc(ft_made, 1)
            pe.wait_ge(d_wq, 16)
            pe.wait_ge(d_wk, 16)

            def fold_heads(g):
                q = slice(DH * (g % 2), DH * (g % 2) + DH)
                for i in range(4):
                    k = 4 * (g // 2) + i
                    last = mm(bank[:, 4 + g % 2, i * D:(i + 1) * D], wqT_sb[q, k], wkT_sb[q, k],
                              start=True, stop=True)
                last.then_inc(a_made, 1)

            pe.wait_ge(ft_sb, 1)
            pe.wait_ge(d_wqkv, 16)
            pe.wait_ge(d_bq, 16)
            pe.wait_ge(d_cst, 16)
            for i in range(3):
                mm(bank[:, 1 + i], wqkv_sb[:, i * D:(i + 1) * D], ft, start=True, stop=False)
                mm(bank[:, 1 + i].rearrange("p (b f) -> p b f", b=B)[:, :, 0],
                   bqkv_sb[0:1, i * D:(i + 1) * D], cst[0:1, LEN0:LEN0 + B], start=False, stop=True
                   ).then_inc(qkv_made, 1)
            fold_heads(0)
            fold_heads(1)
            pe.wait_ge(qk_sb, 1)
            for k in range(2 * B):
                b = k // 2
                last = mm(bank[0:B * FH, 0, 0:M], cst[:, EB0 + 48 - 16 * b:EB0 + 112 - 16 * b],
                          qk[:, k], start=(k == 0), stop=(k == 2 * B - 1))
            last.then_inc(fs_made, 1)
            for c in range(C):
                pe.wait_ge(zc_made, c + 1)
                for b in range(B):
                    last = nc.tensor.transpose(bank[:, 6 + c, b * P:(b + 1) * P], ct[:, c, b], ident)
                last.then_inc(ctxT_made, 1)
            pe.wait_ge(al_made, 1)
            fold_heads(2)
            pe.wait_ge(al_made, 2)
            fold_heads(3)
            pe.wait_ge(fattn_sb, 1)
            for b in range(B):
                last = mm(bank[:, 0, 256 + b * M:256 + (b + 1) * M],
                          cst[0:B * FH, SEL0 + b * P:SEL0 + (b + 1) * P], fattn[:], start=True, stop=True)
            last.then_inc(fab_made, 1)

            def values(g, b, jt, half):
                if g:
                    pe.wait_ge(vl_made, g)
                cols = slice(half * 512, half * 512 + 512)
                keys = slice(jt * P, jt * P + P)
                three(bank[:, V_B], kvh[:, b, keys], kvl[:, b, keys], wvh[:, cols], wvl[:, cols]
                      ).then_inc(v_made, 1)

            pe.wait_ge(wvl_made, 1)
            pe.wait_ge(kvl_made, 2)
            values(0, 0, 0, 0)
            pe.wait_ge(ot_sb, 1)
            pe.wait_ge(d_small, 32)
            for b in range(B):
                mm(bank[:, 1, b * D:(b + 1) * D], ot[:, b].rearrange("p a m -> p (a m)"), wo_sb[:],
                   start=True, stop=False)
                last = mm(bank[:, 1, b * D:(b + 1) * D], ident[0:1, :], bo_sb[:], start=False, stop=True)
            last.then_inc(g_made, 1)
            values(1, 0, 0, 1)
            pe.wait_ge(g_copied, 1)
            for c in range(C):
                mm(bank[:, 2 + c], cst[:, CST0 + c * P:CST0 + (c + 1) * P], g_sb, start=True,
                   stop=True).then_inc(y1_made, 1)
            values(2, 0, 1, 0)
            values(3, 0, 1, 1)
            for b in range(B):
                pe.wait_ge(zl_made, b + 1)
                for c in range(C):
                    last = nc.tensor.transpose(bank[:, LAT_B[b], c * P:(c + 1) * P], zl[:, c, b], ident)
                last.then_inc(latT_made, 1)

            def t_head(n):
                b, h = n // H, n % H
                if n >= 1:
                    pe.wait_ge(tl_made, n)
                three(bank[:, TB_B, 0:S], ah[:, fold_slot(h)], al[:, fold_slot(h)], kvh[:, b, S:J], kvl[:, b, S:J]
                      ).then_inc(t_made, 1)

            pe.wait_ge(al_made, 4)
            pe.wait_ge(kvl_made, 3)
            for n in range(2):
                t_head(n)
            for g, (jt, half) in enumerate([(2, 0), (2, 1), (3, 0), (3, 1)]):
                values(4 + g, 0, jt, half)

            def scores(n, c):
                if n >= 1:
                    pe.wait_ge(exp_made, 2 * (n - 1) + c + 1)
                elif c:
                    pe.wait_ge(kv_made, C + 2)
                b = n // H
                q = slice(c * P, c * P + P)
                three(bank[:, S_B + c], th[:, n % 4, q], tl[:, n % 4, q], kvh[:, b], kvl[:, b]
                      ).then_inc(s_made, 1)

            def transposes(n, c):
                pe.wait_ge(pn_made, 2 * n + c + 1)
                if n >= 1:
                    pe.wait_ge(ptl_made, 2 * (n - 1) + c + 1)
                else:
                    pe.wait_ge(kv_made, C + 3 + c)
                for jt in range(JT):
                    last = nc.tensor.transpose(bank[:, T_B + c, jt * P:(jt + 1) * P],
                                               pr[:, (2 * n + c) % 4, jt * P:(jt + 1) * P], ident)
                last.then_inc(pT_made, 1)

            def attend(n):
                b, h = n // H, n % H
                pe.wait_ge(ptl_made, 2 * n + 2)
                pe.wait_ge(vl_made, 8 * (b + 1))
                if n >= 1:
                    pe.wait_ge(o_sb, n)
                dst = bank[:, O_B, 0:S].rearrange("p (c q) -> p c q", c=C)
                for jt in range(JT):
                    for k, part in enumerate((pth, ptl)):
                        last = mm(dst, vt[:, b % 2, jt, h], part[:, n % 2, :, jt],
                                  start=(jt == 0 and k == 0), stop=(jt == JT - 1 and k == 1))
                last.then_inc(o_made, 1)

            def project(n):
                b, h = n // H, n % H
                pe.wait_ge(o_sb, n + 1)
                if n == 0:
                    pe.wait_ge(d_wo2, 32)
                    pe.wait_ge(kv_made, C + 1)
                if h == 0 and b >= 1:
                    pe.wait_ge(y_used, b)
                for c in range(C):
                    last = mm(bank[:, Y_B, c * D:(c + 1) * D], oT[:, n % 3, c * P:(c + 1) * P],
                              wo2[:, h], start=(h == 0 and c == 0), stop=(h == H - 1),
                              skip_group_check=True)
                last.then_inc(y_part, 1)

            def transpose_x2(b):
                pe.wait_ge(x2_made, b + 1)
                pe.wait_ge(vl_made, v_index(min(ffn_tail(b), NH - H)))
                if b:
                    pe.wait_ge(xT_made, b)
                for c in range(C):
                    last = nc.tensor.transpose(bank[:, V_B, c * P:(c + 1) * P], x2[:, c, b], ident)
                last.then_inc(x2T_made, 1)

            for n in range(STEPS):
                if n < NH:
                    if n == 0:
                        pe.wait_ge(tl_made, 1)
                    else:
                        pe.wait_ge(tl_made, n + 1)
                    if n % H == 0:
                        pe.wait_ge(kvl_made, 2 + n // H + 1)
                    if n == 0:
                        pe.wait_ge(fab_made, 1)
                        pe.wait_ge(ot_sb, 1)
                    scores(n, 0)
                if 1 <= n <= NH:
                    transposes(n - 1, 0)
                if n < NH:
                    scores(n, 1)
                if 1 <= n <= NH:
                    transposes(n - 1, 1)
                if n + 2 < NH:
                    if (n + 2) % H == 0:
                        pe.wait_ge(kvl_made, 2 + (n + 2) // H + 1)
                    t_head(n + 2)
                if 2 <= n < NH + 2:
                    attend(n - 2)
                if v_group(n):
                    b, jt, half = v_group(n)
                    if n % H == 1:
                        pe.wait_ge(kvl_made, 2 + b + 1)
                    if n - 1 in [ffn_tail(k) for k in range(B)]:
                        pe.wait_ge(xT_made, n // H)
                    values(v_index(n), b, jt, half)
                if n >= 3:
                    project(n - 3)
                for b in range(B - 1):
                    if n == ffn_tail(b):
                        transpose_x2(b)

            def router(tiles):
                pe.wait_ge(d_rt, 16)
                for b, c in tiles:
                    k = c * B + b
                    last = mm(bank[:, T_B + (b == B - 1), k * E:(k + 1) * E], xT[:, b, c * P:(c + 1) * P],
                              rt_sb[:], start=True, stop=True)
                last.then_inc(lg_made, 1)

            pe.wait_ge(ptl_made, 2 * NH)
            pe.wait_ge(xT_made, B - 1)
            pe.wait_ge(xTl_made, B - 1)
            pe.wait_ge(wgl_made, E)

            def gate_up(m):
                hf, e = m // E, m % E
                for k, part in enumerate((0, 2, 1, 3)):
                    if m:
                        pe.wait_ge(h_made, 2 * (m - 1) + k // 2 + 1)
                    cols = slice(part * P, part * P + P)
                    w = slice(2 * hf, 2 * hf + 2)
                    three(bank[:, (0, 1, 4, 5)[k]], wgh[:, e, cols], wgl[:, e, cols],
                          xTh[:, w].rearrange("p b s -> p (b s)"),
                          xTl[:, w].rearrange("p b s -> p (b s)")).then_inc(gu_made, 1)

            def down(m):
                e = m % E
                pe.wait_ge(h_made, 2 * m + 2)
                pe.wait_ge(dn_used, m - 1) if m >= 2 else None
                for t in range(4):
                    for k in range(FC):
                        last = mm(bank[:, 6 + m % 2, t * D:(t + 1) * D], hT[:, m % 2, k, t * P:(t + 1) * P],
                                  wd[:, e, k], start=(k == 0), stop=(k == FC - 1))
                last.then_inc(dn_made, 1)

            pe.wait_ge(exp_made, 2 * NH)
            pe.wait_ge(tl_made, NH)
            pe.wait_ge(o_sb, NH)
            gate_up(0)
            router([(b, c) for b in range(B - 1) for c in range(C)])
            transpose_x2(B - 1)
            gate_up(1)
            pe.wait_ge(xT_made, B)
            router([(B - 1, c) for c in range(C)])
            pe.wait_ge(d_wd, 16)
            down(0)
            for m in range(2, 2 * E):
                if m == E:
                    pe.wait_ge(xTl_made, B)
                gate_up(m)
                if m == 2:
                    pe.wait_ge(y_used, B)
                down(m - 1)
            down(2 * E - 1)

        @block.scalar
        def _(act):
            fn = nc.scalar.activation
            act.dma_start(cst[:, 0:256], consts[:, 0:256]).then_inc(d_cs, 16)
            for c in range(C):
                act.dma_start(ct[:, c], ctx_in.rearrange("b (c p) d -> c p b d", p=P)[c]).then_inc(d_ctx, 16)
            act.dma_start(cst[:, 256:], consts[:, 256:]).then_inc(d_cst, 16)
            act.dma_start(ln_sb[:], ln_par).then_inc(d_small, 16)
            act.wait_ge(ft_made, 1)
            fn(ft, bank[:, 0], ACT.Copy).then_inc(ft_sb, 1)

            def fold_hi(g):
                act.wait_ge(a_made, g + 1)
                fn(ah[:, 4 * g:4 * g + 4].rearrange("p h d -> p (h d)"), bank[:, 4 + g % 2], ACT.Copy
                   ).then_inc(ah_made, 1)

            fold_hi(0)
            fold_hi(1)
            act.wait_ge(fnmax_made, 1)
            fn(fexp[:], bank[0:B * FH, 0, 0:M], ACT.Exp, bias=fnmax[:, 0:1], accum_out=fsum[:, 0:1]
               ).then_inc(fexp_made, 1)
            act.wait_ge(d_small, 48)
            for c in range(C):
                act.wait_ge(ctxT_made, c + 1)
                fn(kv[:, :, c * P:(c + 1) * P], bank[:, 6 + c].rearrange("p (b j) -> p b j", b=B),
                   ACT.Identity, bias=ln_sb[:, 1:2], scale=ln_sb[:, 0:1]).then_inc(kv_made, 1)
            act.wait_ge(d_wv, 16)
            fn(wvh[:], wv_sb[:], ACT.Copy).then_inc(wvh_made, 1)
            fold_hi(2)
            fold_hi(3)

            def values_hi(g, b, jt, half):
                act.wait_ge(v_made, g + 1)
                if b >= 2:
                    act.wait_ge(o_made, H * (b - 1))
                fn(vt[:, b % 2, jt, 8 * half:8 * half + 8, 0:DH],
                   bank[:, V_B].rearrange("p (h d) -> p h d", h=8), ACT.Copy, scale=V_SCALE
                   ).then_inc(vh_made, 1)

            values_hi(0, 0, 0, 0)
            act.wait_ge(g_made, 1)
            fn(g_sb, bank[:, 1], ACT.Copy).then_inc(g_copied, 1)
            values_hi(1, 0, 0, 1)
            values_hi(2, 0, 1, 0)
            values_hi(3, 0, 1, 1)
            for b in range(B):
                act.wait_ge(latT_made, b + 1)
                fn(kv[:, b, S:J], bank[:, LAT_B[b], 0:S],
                   ACT.Identity, bias=ln_sb[:, 3:4], scale=ln_sb[:, 2:3]).then_inc(kv_made, 1)

            def t_hi(n):
                act.wait_ge(t_made, n + 1)
                if n >= 4:
                    act.wait_ge(s_made, 2 * (n - 3))
                fn(th[:, n % 4], bank[:, TB_B, 0:S], ACT.Copy, scale=SCALE
                   ).then_inc(th_made, 1)

            t_hi(0)
            t_hi(1)
            for g, (jt, half) in enumerate([(2, 0), (2, 1), (3, 0), (3, 1)]):
                values_hi(4 + g, 0, jt, half)

            def exponent(n, c):
                u = 2 * n + c
                act.wait_ge(max_made, u + 1)
                if n >= 2:
                    act.wait_ge(pT_made, u - 3)
                fn(pr[:, u % 4], bank[:, S_B + c], ACT.Exp, bias=nmax[:, u:u + 1],
                   accum_out=psm[:, u:u + 1]).then_inc(exp_made, 1)

            def probs_hi(n, c):
                act.wait_ge(pT_made, 2 * n + c + 1)
                if n >= 2:
                    act.wait_ge(o_made, n - 1)
                fn(pth[:, n % 2, c].rearrange("p a q -> p (a q)"), bank[:, T_B + c], ACT.Copy,
                   scale=P_SCALE).then_inc(pth_made, 1)

            def out_copy(n):
                act.wait_ge(o_made, n + 1)
                if n >= 3:
                    act.wait_ge(y_part, n - 2)
                fn(oT[:, n % 3], bank[:, O_B, 0:S], ACT.Copy,
                   scale=1.0 / (P_SCALE * V_SCALE)).then_inc(o_sb, 1)

            def x2T_copy(b):
                act.wait_ge(x2T_made, b + 1)
                fn(xT[:, b], bank[:, V_B, 0:S], ACT.Copy).then_inc(xT_made, 1)

            for n in range(STEPS):
                if n < NH:
                    exponent(n, 0)
                if 1 <= n <= NH:
                    probs_hi(n - 1, 0)
                if n < NH:
                    exponent(n, 1)
                if 1 <= n <= NH:
                    probs_hi(n - 1, 1)
                if n + 2 < NH:
                    t_hi(n + 2)
                if 2 <= n < NH + 2:
                    out_copy(n - 2)
                if v_group(n):
                    values_hi(v_index(n), *v_group(n))
                for b in range(B - 1):
                    if n == ffn_tail(b):
                        x2T_copy(b)
            for m in range(2 * E):
                if m == 1:
                    x2T_copy(B - 1)
                if m == 2:
                    act.wait_ge(top_made, 1)
                    fn(ge2[:], top[:, :, 0:2], ACT.Exp, scale=-1.0).then_inc(ge_made, 1)
                for k in range(FC):
                    i = 2 * m + k
                    act.wait_ge(gu_made, 4 * m + 2 * k + 1)
                    if i >= 2:
                        act.wait_ge(h_made, i - 1)
                    fn(sg[:, i % 2], bank[:, (0, 4)[k]], ACT.Silu).then_inc(sg_made, 1)

        @block.gpsimd
        def _(pool):
            pool.wait_ge(d_fr, 16)
            nc.gpsimd.tensor_tensor(fqk[:], fr_sb[:, 0], fr_sb[:, 1], ALU.mult).then_inc(fqk_made, 1)

            def rstd(i, count, tiles):
                pool.wait_ge(ve_made, count)
                if i == 0:
                    pool.wait_ge(d_cst, 16)
                nc.gpsimd.tensor_tensor(rs[:, i, tiles], ve[:, i, tiles],
                                        cst[:, HALF0:HALF0 + 8][:, tiles], ALU.pow).then_inc(rs_made, 1)

            for i in range(3):
                rstd(i, i + 1, slice(0, 8))

            def normalise(n, c):
                u = 2 * n + c
                pool.wait_ge(rcp_made, u + 1)
                nc.gpsimd.tensor_tensor(pr[:, u % 4], pr[:, u % 4],
                                        rcp[:, u:u + 1].to_broadcast([P, J]), ALU.mult
                                        ).then_inc(pn_made, 1)

            for n in range(STEPS):
                if n < NH:
                    normalise(n, 0)
                    normalise(n, 1)
                if 5 <= n < 5 + 2 * E and n % 2:
                    e = (n - 5) // 2
                    pool.wait_ge(wgh_made, e + 1)
                    nc.gpsimd.tensor_tensor(wgl[:, e], wraw[:, e % 2], wgh[:, e], ALU.subtract
                                            ).then_inc(wgl_made, 1)
                for b in range(B - 1):
                    if n == x2_step(b):
                        rstd(3, 4 + b, slice(b, 8, B))
                    if n == ffn_tail(b) + 1:
                        pool.wait_ge(xTh_made, b + 1)
                        nc.gpsimd.tensor_tensor(xTl[:, b], xT[:, b], xTh[:, b], ALU.subtract
                                                ).then_inc(xTl_made, 1)
            b = B - 1
            rstd(3, 4 + b, slice(b, 8, B))
            pool.wait_ge(xTh_made, b + 1)
            nc.gpsimd.tensor_tensor(xTl[:, b], xT[:, b], xTh[:, b], ALU.subtract).then_inc(xTl_made, 1)
            for hf in range(2):
                rstd(4, 4 + B + hf, slice(0, 8))

        @block.vector
        def _(dve):
            v = nc.vector
            own = [0]

            def mark(ins):
                own[0] += 1
                ins.then_inc(dve_own, 1)

            def settle():
                dve.wait_ge(dve_own, own[0])

            def statistics(i, src, tiles):
                for k in tiles:
                    mark(v.bn_stats(st[:, i, k], src[:, k // B, k % B]))
                settle()
                for k in tiles:
                    mark(v.bn_aggr(mv[:, i, k], st[:, i, k]))
                settle()
                ks = slice(tiles[0], 8, tiles[1] - tiles[0])
                v.tensor_scalar(ve[:, i, ks], mv[:, i, ks, 1], EPS, None, ALU.add).then_inc(ve_made, 1)

            def centre(i, dst, src, k):
                return v.tensor_scalar(dst[:, k // B, k % B], src[:, k // B, k % B], mv[:, i, k, 0:1],
                                       rs[:, i, k:k + 1], ALU.subtract, ALU.mult)

            every = list(range(8))
            dve.wait_ge(d_ctx, 32)
            statistics(0, ct, every)
            dve.wait_ge(rs_made, 1)
            for k in every[:B]:
                last = centre(0, ct, ct, k)
            last.then_inc(zc_made, 1)
            both = [P, 2 * B, M]
            dve.wait_ge(qkv_made, 1)
            dve.wait_ge(fqk_made, 1)
            mark(v.tensor_tensor(qw, bank[:, 1].rearrange("p (a m) -> p a m", m=M),
                                 fqk[:].unsqueeze(1).to_broadcast(both), ALU.mult))
            dve.wait_ge(qkv_made, 2)
            settle()
            v.tensor_tensor(qk, bank[:, 2].rearrange("p (a m) -> p a m", m=M), qw, ALU.mult
                            ).then_inc(qk_sb, 1)
            dve.wait_ge(qkv_made, 3)
            dve.wait_ge(d_fr, 16)
            mark(v.tensor_tensor(vw.rearrange("p b a m -> p (b a) m"),
                                 bank[:, 3].rearrange("p (a m) -> p a m", m=M),
                                 fr_sb[:, 2].unsqueeze(1).to_broadcast(both), ALU.mult))
            dve.wait_ge(fs_made, 1)
            v.tensor_reduce(fnmax[:, 0:1], bank[0:B * FH, 0, 0:M], AX_X, ALU.max, negate=True
                            ).then_inc(fnmax_made, 1)
            for k in every[B:]:
                last = centre(0, ct, ct, k)
            last.then_inc(zc_made, 1)

            def fold_lo(g):
                dve.wait_ge(ah_made, g + 1)
                v.tensor_tensor(al[:, 4 * g:4 * g + 4].rearrange("p h d -> p (h d)"), bank[:, 4 + g % 2],
                                ah[:, 4 * g:4 * g + 4].rearrange("p h d -> p (h d)"), ALU.subtract
                                ).then_inc(al_made, 1)

            dve.wait_ge(fexp_made, 1)
            mark(v.reciprocal(frcp[:, 0:1], fsum[:, 0:1]))
            settle()
            v.tensor_scalar(fattn[:], fexp[:], frcp[:, 0:1], None, ALU.mult).then_inc(fattn_sb, 1)
            fold_lo(0)
            fold_lo(1)
            dve.wait_ge(fab_made, 1)
            v.tensor_tensor(ot, vw,
                            bank[:, 0, 256:512].rearrange("p (b m) -> p b m", b=B).unsqueeze(2)
                            .to_broadcast([P, B, 2, M]), ALU.mult).then_inc(ot_sb, 1)

            def split_kv(count, at):
                dve.wait_ge(kv_made, count)
                v.tensor_copy(kvh[at], kv[at]).then_inc(kvh_made, 1)
                dve.wait_ge(kvh_made, count)
                v.tensor_tensor(kvl[at], kv[at], kvh[at], ALU.subtract).then_inc(kvl_made, 1)

            for c in range(C):
                split_kv(c + 1, (slice(None), slice(None), slice(c * P, c * P + P)))
            dve.wait_ge(wvh_made, 1)
            v.tensor_tensor(wvl[:], wv_sb[:], wvh[:], ALU.subtract).then_inc(wvl_made, 1)
            fold_lo(2)
            fold_lo(3)

            def values_lo(g, b, jt, half):
                dve.wait_ge(vh_made, g + 1)
                heads = slice(8 * half, 8 * half + 8)
                v.scalar_tensor_tensor(out=vt[:, b % 2, jt, heads, DH:2 * DH],
                                       in0=bank[:, V_B].rearrange("p (h d) -> p h d", h=8),
                                       scalar=V_SCALE, in1=vt[:, b % 2, jt, heads, 0:DH],
                                       op0=ALU.mult, op1=ALU.subtract).then_inc(vl_made, 1)

            values_lo(0, 0, 0, 0)
            values_lo(1, 0, 0, 1)
            for c in range(C):
                dve.wait_ge(y1_made, c + 1)
                mark(v.tensor_tensor(xt[:, c].rearrange("p b d -> p (b d)"), bank[:, 2 + c],
                                     xt[:, c].rearrange("p b d -> p (b d)"), ALU.add))
            settle()
            statistics(1, xt, every)
            values_lo(2, 0, 1, 0)
            dve.wait_ge(rs_made, 2)
            for k in every:
                mark(centre(1, x1, xt, k))
            settle()
            statistics(2, x1, every)
            values_lo(3, 0, 1, 1)
            dve.wait_ge(rs_made, 3)
            for b in range(B):
                for c in range(C):
                    last = centre(2, zl, x1, c * B + b)
                last.then_inc(zl_made, 1)
            split_kv(3, (slice(None), 0, slice(S, J)))

            def t_lo(n):
                dve.wait_ge(th_made, n + 1)
                v.scalar_tensor_tensor(out=tl[:, n % 4], in0=bank[:, TB_B, 0:S],
                                       scalar=SCALE, in1=th[:, n % 4].bitcast(F32), op0=ALU.mult,
                                       op1=ALU.subtract).then_inc(tl_made, 1)

            t_lo(0)
            t_lo(1)
            for g, (jt, half) in enumerate([(2, 0), (2, 1), (3, 0), (3, 1)]):
                values_lo(4 + g, 0, jt, half)
            for b in range(1, B):
                split_kv(3 + b, (slice(None), b, slice(S, J)))

            def row_max(n, c):
                u = 2 * n + c
                dve.wait_ge(s_made, u + 1)
                v.tensor_reduce(nmax[:, u:u + 1], bank[:, S_B + c], AX_X, ALU.max, negate=True
                                ).then_inc(max_made, 1)

            def sum_reciprocal(n, c):
                u = 2 * n + c
                dve.wait_ge(exp_made, u + 1)
                v.reciprocal(rcp[:, u:u + 1], psm[:, u:u + 1]).then_inc(rcp_made, 1)

            def probs_lo(n, c):
                dve.wait_ge(pth_made, 2 * n + c + 1)
                v.scalar_tensor_tensor(out=ptl[:, n % 2, c].rearrange("p a q -> p (a q)"),
                                       in0=bank[:, T_B + c], scalar=P_SCALE,
                                       in1=pth[:, n % 2, c].rearrange("p a q -> p (a q)"),
                                       op0=ALU.mult, op1=ALU.subtract).then_inc(ptl_made, 1)

            def second_norm_in(b):
                dve.wait_ge(y_part, H * (b + 1))
                ins = v.tensor_tensor(acc[:, :, b], bank[:, Y_B, 0:C * D].rearrange(
                    "p (c d) -> p c d", c=C), x1[:, :, b], ALU.add)
                ins.then_inc(y_used, 1)
                dve.wait_ge(y_used, b + 1)
                statistics(3, acc, [b, B + b])

            def second_norm_out(b):
                dve.wait_ge(rs_made, 4 + b)
                for c in range(C):
                    last = centre(3, x2, acc, c * B + b)
                last.then_inc(x2_made, 1)

            def split_x2T(b):
                dve.wait_ge(xT_made, b + 1)
                v.tensor_copy(xTh[:, b], xT[:, b]).then_inc(xTh_made, 1)

            for n in range(STEPS):
                if n < NH:
                    row_max(n, 0)
                if 1 <= n <= NH:
                    probs_lo(n - 1, 0)
                if n < NH:
                    row_max(n, 1)
                for b in range(B - 1):
                    if n == x2_step(b):
                        second_norm_in(b)
                if n < NH:
                    sum_reciprocal(n, 0)
                if 1 <= n <= NH:
                    probs_lo(n - 1, 1)
                if n + 2 < NH:
                    t_lo(n + 2)
                if n < NH:
                    sum_reciprocal(n, 1)
                if v_group(n):
                    values_lo(v_index(n), *v_group(n))
                if 4 <= n < 4 + 2 * E and n % 2 == 0:
                    e = (n - 4) // 2
                    dve.wait_ge(d_raw[e % 2], 16 * (e // 2 + 1))
                    v.tensor_copy(wgh[:, e], wraw[:, e % 2]).then_inc(wgh_made, 1)
                for b in range(B - 1):
                    if n == x2_step(b) + 1:
                        second_norm_out(b)
                    if n == ffn_tail(b):
                        split_x2T(b)
            second_norm_in(B - 1)
            second_norm_out(B - 1)
            def hidden(m):
                for k in range(FC):
                    i = 2 * m + k
                    dve.wait_ge(sg_made, i + 1)
                    dve.wait_ge(gu_made, 4 * m + 2 * k + 2)
                    if m >= 2:
                        dve.wait_ge(dn_made, m - 1)
                    v.tensor_tensor(hT[:, m % 2, k], bank[:, (1, 5)[k]], sg[:, i % 2], ALU.mult
                                    ).then_inc(h_made, 1)

            def accumulate(m):
                hf, e = m // E, m % E
                dve.wait_ge(dn_made, m + 1)
                settle()
                for t in range(4):
                    b, c = 2 * hf + t // C, t % C
                    k = c * B + b
                    last = v.scalar_tensor_tensor(out=acc[:, c, b], in0=bank[:, 6 + m % 2, t * D:(t + 1) * D],
                                                  scalar=gate[:, k, e:e + 1],
                                                  in1=(x2 if e == 0 else acc)[:, c, b],
                                                  op0=ALU.mult, op1=ALU.add)
                    mark(last) if t < 3 else last.then_inc(dn_used, 1)
                dve.wait_ge(dn_used, m + 1)

            def last_norm(hf):
                settle()
                tiles = [c * B + 2 * hf + i for c in range(C) for i in range(2)]
                for k in tiles:
                    mark(v.bn_stats(st[:, 4, k], acc[:, k // B, k % B]))
                settle()
                for k in tiles:
                    mark(v.bn_aggr(mv[:, 4, k], st[:, 4, k]))
                settle()
                if hf == 0:
                    mark(v.memset(ve[:, 4], 1.0))
                    settle()
                for c in range(C):
                    ks = slice(c * B + 2 * hf, c * B + 2 * hf + 2)
                    ins = v.tensor_scalar(ve[:, 4, ks], mv[:, 4, ks, 1], EPS, None, ALU.add)
                    mark(ins) if c == 0 else ins.then_inc(ve_made, 1)
                settle()
                dve.wait_ge(rs_made, 3 + B + hf + 1)
                for k in tiles:
                    centre(4, acc, acc, k).then_inc(fin_made, 1)

            hidden(0)
            split_x2T(B - 1)
            hidden(1)
            dve.wait_ge(lg_made, 1)
            dve.wait_ge(lg_made, 2)
            lgs = [bank[:, T_B + i, 0:8 * E].rearrange("p (c b e) -> p c b e", c=C, b=B) for i in (0, 1)]
            lg4 = lg[:].rearrange("p (c b) e -> p c b e", c=C)
            mark(v.tensor_copy(lg4[:, :, 0:B - 1], lgs[0][:, :, 0:B - 1]))
            mark(v.tensor_copy(lg4[:, :, B - 1], lgs[1][:, :, B - 1]))
            settle()
            for k in every:
                ins = v.max(top[:, k], lg[:, k])
                mark(ins)
            settle()
            for k in every:
                mark(v.max_index(topi[:, k], top[:, k], lg[:, k]))
            settle()
            mark(v.tensor_copy(topf[:], topi[:]))
            settle()
            v.tensor_copy(m0[:, 0, 0:1], topf[:, 0, 0:1]).then_inc(top_made, 1)
            dve.wait_ge(ge_made, 1)
            mark(v.tensor_scalar(gn[:], ge2[:], 1.0, None, ALU.add))
            settle()
            mark(v.reciprocal(ge2[:], gn[:]))
            settle()
            mark(v.tensor_tensor(gs[:], ge2[:, :, 0], ge2[:, :, 1], ALU.add))
            settle()
            mark(v.tensor_scalar(gs[:], gs[:], 1e-10, None, ALU.add))
            settle()
            mark(v.reciprocal(gr[:], gs[:]))
            settle()
            mark(v.tensor_tensor(gn[:], ge2[:], gr[:].unsqueeze(2).to_broadcast([P, 8, 2]), ALU.mult))
            iota = cst[:, IO0:IO0 + 64].rearrange("p (k e) -> p k e", e=E)
            wide = [P, 8, E]
            mark(v.tensor_tensor(m0[:], iota, topf[:, :, 0:1].to_broadcast(wide), ALU.is_equal))
            mark(v.tensor_tensor(m1[:], iota, topf[:, :, 1:2].to_broadcast(wide), ALU.is_equal))
            settle()
            mark(v.tensor_tensor(m0[:], m0[:], gn[:, :, 0:1].to_broadcast(wide), ALU.mult))
            mark(v.tensor_tensor(m1[:], m1[:], gn[:, :, 1:2].to_broadcast(wide), ALU.mult))
            settle()
            mark(v.tensor_tensor(gate[:], m0[:], m1[:], ALU.add))
            settle()

            for m in range(1, 2 * E):
                if m > 1:
                    hidden(m)
                accumulate(m - 1)
                if m - 1 == E - 1:
                    last_norm(0)
            accumulate(2 * E - 1)
            last_norm(1)


def constants():
    import numpy as np
    k = np.zeros((P, NCONST), np.float32)
    s, f = np.arange(S)[:, None], np.arange(M)[None, :]
    angle = 2 * np.pi * ((s * f) % S) / S
    cs = np.concatenate([np.cos(angle), np.sin(angle)], 1).astype(np.float32)
    for c in range(C):
        k[:, CS0 + c * P:CS0 + (c + 1) * P] = cs[c * P:(c + 1) * P]
    k[:, CST0:CST0 + S] = cs.T
    k[:, ID0:ID0 + P] = np.eye(P)
    for p in range(P):
        k[p, EB0 + 48 + p // HD] = 1
        for b in range(B):
            k[16 * b + p // HD, SEL0 + b * P + p] = 1
    k[:, IO0:IO0 + 64] = np.tile(np.arange(E), 8)
    k[:, HALF0:HALF0 + 8] = -0.5
    k[:, LEN0:LEN0 + B] = S
    return k


def kernel(**inputs):
    import numpy as np
    import concourse.bacc as bacc
    from concourse.bass_utils import run_bass_kernel_spmd

    a = {n: np.asarray(v) for n, v in inputs.items()}
    inner = H * DH
    wkv = a["L0_xattn_Wkv"]
    arrays = {
        "x": a["x"],
        "ctx_in": a["ctx_1024"],
        "w_qkvT": a["L0_attn_w_qkv"].T,
        "b_qkv": a["L0_attn_b_qkv"][None],
        "w_outT": a["L0_attn_w_out"].T,
        "b_out": a["L0_attn_b_out"][None],
        "freqT": np.concatenate([a[f"L0_attn_freq_{n}"].transpose(0, 2, 1).reshape(D, M) for n in "qkv"], 1),
        "ln_par": np.stack([a[f"L0_xattn_ln_{n}"] for n in ("m_g", "m_b", "l_g", "l_b")], 1),
        "wqT": a["L0_xattn_Wq"].T,
        "wkT": wkv[:, :inner].T,
        "wv": wkv[:, inner:],
        "wout": a["L0_xattn_Wout"],
        "routerT": a["L0_ffn_router_w"].T,
        "w_gu": np.concatenate([a["L0_ffn_w_gate"], a["L0_ffn_w_up"]], 2).transpose(1, 0, 2),
        "w_down": a["L0_ffn_w_down"],
        "consts": constants(),
    }
    arrays = {n: np.ascontiguousarray(v) for n, v in arrays.items()}
    nc = bacc.Bacc("TRN2", target_bir_lowering=False, num_devices=1)
    args = [nc.dram_tensor(f"in_{n}", v.shape, mybir.dt.from_np(v.dtype), kind="ExternalInput").ap()
            for n, v in arrays.items()]
    out = nc.dram_tensor("out", (B, S, D), F32, kind="ExternalOutput").ap()
    decoder_layer(nc, *args, out)
    r = run_bass_kernel_spmd(nc, [{f"in_{n}": v for n, v in arrays.items()}], core_ids=[0])
    return r.results[0]["out"]
```

```python
from contextlib import ExitStack

import concourse.bass as bass
from concourse import mybir

F32 = mybir.dt.float32
F32R = mybir.dt.float32r
F16 = mybir.dt.float16
U32 = mybir.dt.uint32
ALU = mybir.AluOpType
ACT = mybir.ActivationFunctionType
AX_X = mybir.AxisListType.X

P = 128
D = 128
B = 4
S = 256
C = S // P
M = 64
FH = 16
HD = D // FH
H = 16
DH = 64
J = 2 * S
JT = J // P
NH = B * H
E = 8
F = 256
FC = F // P
EPS = 1e-5
SCALE = DH ** -0.5
P_SCALE = 1024.0
V_SCALE = 64.0

CS0, CST0, ID0, EB0, SEL0, IO0, HALF0, LEN0, NCONST = 0, 256, 512, 640, 752, 1264, 1328, 1336, 1340


def decoder_layer(nc, x, ctx_in, w_qkvT, b_qkv, w_outT, b_out, freqT, ln_par, wqT, wkT, wv, wout,
                  routerT, w_gu, w_down, consts, out):
    with ExitStack() as ctx:
        def sb(name, shape, dt=F32):
            return ctx.enter_context(nc.sbuf_tensor(name, shape, dt))

        def sem(name):
            return ctx.enter_context(nc.semaphore(name))

        cst = sb("cst", [P, NCONST])
        xt = sb("xt", [P, C, B, D])
        ct = sb("ct", [P, C, B, D])
        x1 = sb("x1", [P, C, B, D])
        zl = sb("zl", [P, C, B, D])
        x2 = zl
        acc = xt
        wqkv_sb = sb("wqkv_sb", [P, 3 * D])
        bqkv_sb = sb("bqkv_sb", [1, 3 * D])
        wo_sb = sb("wo_sb", [P, D])
        bo_sb = sb("bo_sb", [1, D])
        fr_sb = sb("fr_sb", [P, 3, M])
        ln_sb = sb("ln_sb", [P, 4])
        wqk_sb = sb("wqk_sb", [P, 2, H // 2, D])
        wqT_sb, wkT_sb = wqk_sb[:, 0], wqk_sb[:, 1]
        wv_sb = sb("wv_sb", [P, H * DH])
        wvh = sb("wvh", [P, H * DH], F32R)
        wvl = sb("wvl", [P, H * DH], F32R)
        wo2 = sb("wo2", [P, H, D])
        rt_sb = sb("rt_sb", [P, E])
        work = sb("work", [P, 6, 512])
        ft = work[:, 0]
        fqk = sb("fqk", [P, M])
        qw = work[:, 1].rearrange("p (k m) -> p k m", m=M)
        qk = work[:, 2].rearrange("p (k m) -> p k m", m=M)
        vw = work[:, 3].rearrange("p (b a m) -> p b a m", b=B, a=2)
        ot = work[:, 4].rearrange("p (b a m) -> p b a m", b=B, a=2)
        fnmax = sb("fnmax", [B * FH, 1])
        fexp = sb("fexp", [B * FH, M])
        fsum = sb("fsum", [B * FH, 1])
        frcp = sb("frcp", [B * FH, 1])
        fattn = sb("fattn", [B * FH, M])
        g_sb = work[:, 5]
        st = sb("st", [P, 5, C * B, 6])
        mv = sb("mv", [P, 5, C * B, 2])
        ve = sb("ve", [P, 5, C * B])
        rs = sb("rs", [P, 5, C * B])
        ah = sb("ah", [P, H, D], F32R)
        al = sb("al", [P, H, D], F32R)
        kv = sb("kv", [P, B, J])
        kvh = sb("kvh", [P, B, J], F32R)
        kvl = sb("kvl", [P, B, J], F32R)
        th = sb("th", [P, 4, S], F32R)
        tl = sb("tl", [P, 4, S], F32R)
        vt = sb("vt", [P, 2, JT, H, 2 * DH], F16)
        pr = wqk_sb[:].rearrange("p a k d -> p (a k d)").rearrange("p (i j) -> p i j", i=4)
        nmax = sb("nmax", [P, 2 * NH])
        psm = sb("psm", [P, 2 * NH])
        rcp = sb("rcp", [P, 2 * NH])
        pth = sb("pth", [P, 2, C, JT, P], F16)
        ptl = sb("ptl", [P, 2, C, JT, P], F16)
        oT = sb("oT", [P, 3, S])
        wraw = ct[:].rearrange("p c b d -> p c (b d)")
        wgh = sb("wgh", [P, E, 2 * F], F32R)
        wgl = sb("wgl", [P, E, 2 * F], F32R)
        wd = kv[:].rearrange("p b j -> p (b j)").rearrange("p (e k n) -> p e k n", e=E, k=FC)
        xT = wv_sb[:].rearrange("p (b s) -> p b s", b=B)
        xTh = sb("xTh", [P, B, S], F32R)
        xTl = sb("xTl", [P, B, S], F32R)
        lg = sb("lg", [P, 8, E])
        top = sb("top", [P, 8, 8])
        topi = sb("topi", [P, 8, 8], U32)
        topf = sb("topf", [P, 8, 8])
        ge2 = sb("ge2", [P, 8, 2])
        gs = sb("gs", [P, 8])
        gr = sb("gr", [P, 8])
        gn = sb("gn", [P, 8, 2])
        m0 = sb("m0", [P, 8, E])
        m1 = sb("m1", [P, 8, E])
        gate = sb("gate", [P, 8, E])
        sg = work[:, 0:2]
        hT = work[:, 2:6].rearrange("p (i k) t -> p i k t", k=FC)

        bank = ctx.enter_context(nc.psum_tensor("bank", [P, 8, 512], F32))
        S_B, T_B, O_B, TB_B, V_B, Y_B = 0, 2, 4, 5, 6, 7
        GU_B = (0, 1, 2, 3)
        DN_B = (5, 6)

        ident = cst[:, ID0:ID0 + P]

        (d_x, d_cs, d_cst, d_ctx, d_wqkv, d_bq, d_fr, d_wo, d_ln, d_wq, d_wk, d_wv, d_wo2, d_rt,
         d_wd, d_out) = [sem(n) for n in (
            "d_x", "d_cs", "d_cst", "d_ctx", "d_wqkv", "d_bq", "d_fr", "d_wo", "d_ln", "d_wq", "d_wk",
            "d_wv", "d_wo2", "d_rt", "d_wd", "d_out")]
        d_raw = [sem("d_raw0"), sem("d_raw1")]
        ft_made, ft_sb, qkv_made, fqk_made, qk_sb, vw_sb, fs_made, fnmax_made, fexp_made = [
            sem(n) for n in ("ft_made", "ft_sb", "qkv_made", "fqk_made", "qk_sb", "vw_sb",
                             "fs_made", "fnmax_made", "fexp_made")]
        fattn_sb, fab_made, ot_sb, g_made, g_copied, y1_made, a_made, ah_made, al_made = [
            sem(n) for n in ("fattn_sb", "fab_made", "ot_sb", "g_made", "g_copied", "y1_made",
                             "a_made", "ah_made", "al_made")]
        zc_made, ctxT_made, kv_made, kvh_made, kvl_made, zl_made, latT_made = [
            sem(n) for n in ("zc_made", "ctxT_made", "kv_made", "kvh_made", "kvl_made", "zl_made",
                             "latT_made")]
        wvh_made, wvl_made, v_made, vh_made, vl_made, t_made, th_made, tl_made = [
            sem(n) for n in ("wvh_made", "wvl_made", "v_made", "vh_made", "vl_made", "t_made",
                             "th_made", "tl_made")]
        s_made, max_made, exp_made, rcp_made, pn_made, pT_made, pth_made, ptl_made = [
            sem(n) for n in ("s_made", "max_made", "exp_made", "rcp_made", "pn_made", "pT_made",
                             "pth_made", "ptl_made")]
        o_made, o_sb, y_part, y_used, x2_made, x2T_made, xT_made, xTh_made, xTl_made = [
            sem(n) for n in ("o_made", "o_sb", "y_part", "y_used", "x2_made", "x2T_made",
                             "xT_made", "xTh_made", "xTl_made")]
        ve_made, rs_made, wgh_made, wgl_made = [
            sem(n) for n in ("ve_made", "rs_made", "wgh_made", "wgl_made")]
        lg_made, lg_copied, top_made, ge_made, gate_made = [
            sem(n) for n in ("lg_made", "lg_copied", "top_made", "ge_made", "gate_made")]
        gu_made, sg_made, h_made, dn_made, dn_used, fin_made = [
            sem(n) for n in ("gu_made", "sg_made", "h_made", "dn_made", "dn_used", "fin_made")]
        dve_own = sem("dve_own")

        STEPS = NH + 3

        def fold_slot(h):
            return 4 * (2 * (h // 8) + h % 2) + h % 8 // 2

        V_GROUPS = [(b, jt, half) for b in range(B) for jt in range(JT) for half in range(2)]
        V_EARLY = 2 * C
        v_at = {}
        for g in range(V_EARLY, 8 * B):
            at = g - V_EARLY if g < 8 else 2 * (H * (g // 8 - 1) + 2 * (g % 8) + 1) + 1
            v_at.setdefault(at, []).append(g)

        G_TILES = (slice(0, C * (B - 1)), slice(C * (B - 1), C * B))

        def v_bank(g):
            return V_B + (g % 2 if g < 8 else 0)

        def v_before(u):
            return V_EARLY + sum(len(gs) for at, gs in v_at.items() if at < u)

        def lat_at(b, piece):
            return 2 * H * (b - 1) + dict(stats=0, var=1, norm1=5, stats2=6, var2=7, norm2=11,
                                          turn=13, split=15)[piece]

        def x2_at(b, piece):
            return 2 * H * (b + 1) + dict(add=5, stats=7, var=8, norm=13, turn=17, split=19)[piece]

        ROUTE_AT = x2_at(B - 2, "turn") + 4
        LAST_NORM = B - 1

        block = ctx.enter_context(nc.Block())

        @block.sync
        def _(sp):
            for c in range(C):
                sp.dma_start(xt[:, c], x.rearrange("b (c p) d -> c p b d", p=P)[c]).then_inc(d_x, 16)
            sp.dma_start(wqkv_sb[:], w_qkvT).then_inc(d_wqkv, 16)
            sp.dma_start(bqkv_sb[:], b_qkv).then_inc(d_bq, 16)
            sp.dma_start(fr_sb[:], freqT.rearrange("p (a m) -> p a m", a=3)).then_inc(d_fr, 16)
            sp.dma_start(wqT_sb, wqT.rearrange("(k p) d -> p k d", p=P)).then_inc(d_wq, 16)
            sp.dma_start(wkT_sb, wkT.rearrange("(k p) d -> p k d", p=P)).then_inc(d_wk, 16)
            sp.dma_start(wo_sb[:], w_outT).then_inc(d_wo, 16)
            sp.dma_start(bo_sb[:], b_out).then_inc(d_wo, 16)
            sp.dma_start(wv_sb[:], wv).then_inc(d_wv, 16)
            for r in range(2):
                sp.dma_start(wo2[r * DH:(r + 1) * DH], wout.rearrange("(h q) n -> q h n", q=DH)
                             ).then_inc(d_wo2, 16)
            sp.dma_start(rt_sb[:], routerT).then_inc(d_rt, 16)
            sp.wait_ge(ctxT_made, 2)
            for e in range(E):
                if e >= 2:
                    sp.wait_ge(wgl_made, e - 1)
                sp.dma_start(wraw[:, e % 2], w_gu[:, e]).then_inc(d_raw[e % 2], 16)
            sp.wait_ge(kvl_made, C + B)
            sp.wait_ge(kvh_made, C + B)
            sp.dma_start(wd, w_down.rearrange("e (c p) n -> p e c n", p=P)).then_inc(d_wd, 16)
            for hf in range(2):
                sp.wait_ge(fin_made, 4 * (hf + 1))
                for c in range(C):
                    sp.dma_start(out.rearrange("b (c p) d -> c p b d", p=P)[c, :, 2 * hf:2 * hf + 2],
                                 acc[:, c, 2 * hf:2 * hf + 2]).then_inc(d_out, 16)
            sp.wait_ge(d_out, 16 * 2 * C)

        @block.tensor
        def _(pe):
            mm = nc.tensor.matmul

            def three(dst, wh, wl, mh, ml):
                mm(dst, wh, mh, start=True, stop=False)
                mm(dst, wh, ml, start=False, stop=False)
                return mm(dst, wl, mh, start=False, stop=True)

            pe.wait_ge(d_x, 32)
            pe.wait_ge(d_cs, 16)
            for b in range(B):
                for c in range(C):
                    last = mm(bank[:, 0, b * P:(b + 1) * P], xt[:, c, b],
                              cst[:, CS0 + c * P:CS0 + (c + 1) * P], start=(c == 0), stop=(c == C - 1))
            last.then_inc(ft_made, 1)
            pe.wait_ge(d_wq, 16)
            pe.wait_ge(d_wk, 16)

            def fold_heads(g):
                q = slice(DH * (g % 2), DH * (g % 2) + DH)
                for i in range(4):
                    k = 4 * (g // 2) + i
                    last = mm(bank[:, 4 + g % 2, i * D:(i + 1) * D], wqT_sb[q, k], wkT_sb[q, k],
                              start=True, stop=True)
                last.then_inc(a_made, 1)

            pe.wait_ge(ft_sb, 1)
            pe.wait_ge(d_wqkv, 16)
            pe.wait_ge(d_bq, 16)
            pe.wait_ge(d_cst, 16)
            for i in range(3):
                mm(bank[:, 1 + i], wqkv_sb[:, i * D:(i + 1) * D], ft, start=True, stop=False)
                mm(bank[:, 1 + i].rearrange("p (b f) -> p b f", b=B)[:, :, 0],
                   bqkv_sb[0:1, i * D:(i + 1) * D], cst[0:1, LEN0:LEN0 + B], start=False, stop=True
                   ).then_inc(qkv_made, 1)
            fold_heads(0)
            fold_heads(1)
            pe.wait_ge(qk_sb, 1)
            for k in range(2 * B):
                b = k // 2
                last = mm(bank[0:B * FH, 0, 0:M], cst[:, EB0 + 48 - 16 * b:EB0 + 112 - 16 * b],
                          qk[:, k], start=(k == 0), stop=(k == 2 * B - 1))
            last.then_inc(fs_made, 1)
            def context_T(c):
                pe.wait_ge(zc_made, c + 1)
                for b in range(B):
                    last = nc.tensor.transpose(bank[:, 6 + c, b * P:(b + 1) * P], ct[:, c, b], ident)
                last.then_inc(ctxT_made, 1)

            context_T(0)
            pe.wait_ge(fattn_sb, 1)
            for b in range(B):
                last = mm(bank[:, 0, 256 + b * M:256 + (b + 1) * M],
                          cst[0:B * FH, SEL0 + b * P:SEL0 + (b + 1) * P], fattn[:], start=True, stop=True)
            last.then_inc(fab_made, 1)
            context_T(1)
            pe.wait_ge(ot_sb, 1)
            pe.wait_ge(d_wo, 32)
            for b in range(B):
                mm(bank[:, 1, b * D:(b + 1) * D], ot[:, b].rearrange("p a m -> p (a m)"), wo_sb[:],
                   start=True, stop=False)
                last = mm(bank[:, 1, b * D:(b + 1) * D], ident[0:1, :], bo_sb[:], start=False, stop=True)
            last.then_inc(g_made, 1)
            pe.wait_ge(g_copied, 1)
            for c in range(C):
                mm(bank[:, 2 + c], cst[:, CST0 + c * P:CST0 + (c + 1) * P], g_sb, start=True,
                   stop=True).then_inc(y1_made, 1)
            pe.wait_ge(al_made, 1)
            fold_heads(2)
            pe.wait_ge(al_made, 2)
            fold_heads(3)

            def values(g):
                b, jt, half = V_GROUPS[g]
                if g >= 2:
                    pe.wait_ge(vl_made, g - 1 if g <= 8 else g)
                cols = slice(half * 512, half * 512 + 512)
                keys = slice(jt * P, jt * P + P)
                three(bank[:, v_bank(g)], kvh[:, b, keys], kvl[:, b, keys], wvh[:, cols], wvl[:, cols]
                      ).then_inc(v_made, 1)

            def latents_T(b):
                pe.wait_ge(zl_made, b + 1)
                for c in range(C):
                    last = nc.tensor.transpose(bank[:, TB_B if b == 0 else V_B, c * P:(c + 1) * P],
                                               zl[:, c, b], ident)
                last.then_inc(latT_made, 1)

            pe.wait_ge(wvl_made, 1)
            for g in range(V_EARLY):
                pe.wait_ge(kvl_made, g // 2 + 1)
                values(g)
            pe.wait_ge(al_made, 4)
            latents_T(0)

            def t_head(n):
                b, h = n // H, n % H
                if n >= 1:
                    pe.wait_ge(tl_made, n)
                three(bank[:, TB_B, 0:S], ah[:, fold_slot(h)], al[:, fold_slot(h)], kvh[:, b, S:J], kvl[:, b, S:J]
                      ).then_inc(t_made, 1)

            pe.wait_ge(kvl_made, C + 1)
            for n in range(2):
                t_head(n)

            def scores(n, c):
                if n >= 1:
                    pe.wait_ge(exp_made, 2 * (n - 1) + c + 1)
                b = n // H
                q = slice(c * P, c * P + P)
                three(bank[:, S_B + c], th[:, n % 4, q], tl[:, n % 4, q], kvh[:, b], kvl[:, b]
                      ).then_inc(s_made, 1)

            def transposes(n, c):
                pe.wait_ge(pn_made, 2 * n + c + 1)
                if n >= 1:
                    pe.wait_ge(ptl_made, 2 * (n - 1) + c + 1)
                for jt in range(JT):
                    last = nc.tensor.transpose(bank[:, T_B + c, jt * P:(jt + 1) * P],
                                               pr[:, (2 * n + c) % 4, jt * P:(jt + 1) * P], ident)
                last.then_inc(pT_made, 1)

            def attend(n):
                b, h = n // H, n % H
                pe.wait_ge(ptl_made, 2 * n + 2)
                pe.wait_ge(vl_made, 8 * (b + 1))
                if n >= 1:
                    pe.wait_ge(o_sb, n)
                dst = bank[:, O_B, 0:S].rearrange("p (c q) -> p c q", c=C)
                for jt in range(JT):
                    for k, part in enumerate((pth, ptl)):
                        last = mm(dst, vt[:, b % 2, jt, h], part[:, n % 2, :, jt],
                                  start=(jt == 0 and k == 0), stop=(jt == JT - 1 and k == 1))
                last.then_inc(o_made, 1)

            def project(n):
                b, h = n // H, n % H
                pe.wait_ge(o_sb, n + 1)
                if n == 0:
                    pe.wait_ge(d_wo2, 32)
                    pe.wait_ge(vl_made, 8)
                if h == 0 and b >= 1:
                    pe.wait_ge(y_used, b)
                for c in range(C):
                    last = mm(bank[:, Y_B, c * D:(c + 1) * D], oT[:, n % 3, c * P:(c + 1) * P],
                              wo2[:, h], start=(h == 0 and c == 0), stop=(h == H - 1),
                              skip_group_check=True)
                last.then_inc(y_part, 1)

            def transpose_x2(b):
                pe.wait_ge(x2_made, b + 1)
                pe.wait_ge(vl_made, v_before(x2_at(b, "turn")))
                for c in range(C):
                    last = nc.tensor.transpose(bank[:, V_B, c * P:(c + 1) * P], x2[:, c, b], ident)
                last.then_inc(x2T_made, 1)

            def router(tiles):
                pe.wait_ge(d_rt, 16)
                for b, c in tiles:
                    k = C * b + c
                    last = mm(bank[:, V_B, k * E:(k + 1) * E], xT[:, b, c * P:(c + 1) * P],
                              rt_sb[:], start=True, stop=True)
                last.then_inc(lg_made, 1)

            def gate_up(m, ks):
                hf, e = m // E, m % E
                for k in ks:
                    part = (0, 2, 1, 3)[k]
                    if m:
                        pe.wait_ge(h_made, 2 * (m - 1) + k // 2 + 1)
                    cols = slice(part * P, part * P + P)
                    w = slice(2 * hf, 2 * hf + 2)
                    three(bank[:, GU_B[k]], wgh[:, e, cols], wgl[:, e, cols],
                          xTh[:, w].rearrange("p b s -> p (b s)"),
                          xTl[:, w].rearrange("p b s -> p (b s)")).then_inc(gu_made, 1)

            for u in range(2 * STEPS):
                n, c = u // 2, u % 2
                if 0 <= u - 3 < 2 * NH:
                    transposes((u - 3) // 2, (u - 3) % 2)
                if n < NH:
                    pe.wait_ge(tl_made, n + 1)
                    if n % H == 0:
                        pe.wait_ge(kvl_made, C + n // H + 1)
                    scores(n, c)
                if c == 0 and n >= 3:
                    project(n - 3)
                if c == 0 and n + 2 < NH:
                    if (n + 2) % H == 0:
                        pe.wait_ge(kvl_made, C + (n + 2) // H + 1)
                    t_head(n + 2)
                if c == 1 and 2 <= n < NH + 2:
                    attend(n - 2)
                for g in v_at.get(u, []):
                    b, jt, half = V_GROUPS[g]
                    if jt >= C:
                        pe.wait_ge(kvl_made, C + b + 1)
                    for k in range(B):
                        if k < B - 1 and u - 2 == x2_at(k, "turn"):
                            pe.wait_ge(xT_made, k + 1)
                        if k and u - 2 == lat_at(k, "turn"):
                            pe.wait_ge(kv_made, C + k + 1)
                    values(g)
                for b in range(B):
                    if b and u == lat_at(b, "turn"):
                        pe.wait_ge(vl_made, v_before(u))
                        latents_T(b)
                    if b < LAST_NORM and u == x2_at(b, "turn"):
                        transpose_x2(b)
                if u == ROUTE_AT:
                    pe.wait_ge(xT_made, LAST_NORM)
                    pe.wait_ge(vl_made, 8 * B)
                    router([(b, c) for b in range(LAST_NORM) for c in range(C)])
                if u == 2 * NH + 2:
                    pe.wait_ge(xTl_made, 2)
                    pe.wait_ge(wgl_made, E)
                    pe.wait_ge(exp_made, 2 * NH)
                    gate_up(0, (0, 1))
                if u == 2 * NH + 3:
                    pe.wait_ge(ptl_made, 2 * NH)
                    gate_up(0, (2, 3))

            def down(m):
                e = m % E
                pe.wait_ge(h_made, 2 * m + 2)
                if m >= 2:
                    pe.wait_ge(dn_used, m - 1)
                for t in range(4):
                    for k in range(FC):
                        last = mm(bank[:, DN_B[m % 2], t * D:(t + 1) * D], hT[:, m % 2, k, t * P:(t + 1) * P],
                                  wd[:, e, k], start=(k == 0), stop=(k == FC - 1))
                last.then_inc(dn_made, 1)

            gate_up(1, range(4))
            pe.wait_ge(lg_copied, 1)
            transpose_x2(B - 1)
            pe.wait_ge(d_wd, 16)
            pe.wait_ge(tl_made, NH)
            down(0)
            pe.wait_ge(xT_made, B)
            router([(B - 1, c) for c in range(C)])
            gate_up(2, range(4))
            pe.wait_ge(lg_copied, 2)
            down(1)
            for m in range(3, 2 * E):
                if m == E:
                    pe.wait_ge(xTl_made, B)
                gate_up(m, range(4))
                down(m - 1)
            down(2 * E - 1)

        @block.scalar
        def _(act):
            fn = nc.scalar.activation
            act.dma_start(cst[:, 0:256], consts[:, 0:256]).then_inc(d_cs, 16)
            for c in range(C):
                act.dma_start(ct[:, c], ctx_in.rearrange("b (c p) d -> c p b d", p=P)[c]).then_inc(d_ctx, 16)
            act.dma_start(cst[:, 256:], consts[:, 256:]).then_inc(d_cst, 16)
            act.dma_start(ln_sb[:], ln_par).then_inc(d_ln, 16)
            act.wait_ge(ft_made, 1)
            fn(ft, bank[:, 0], ACT.Copy).then_inc(ft_sb, 1)

            def fold_hi(g):
                act.wait_ge(a_made, g + 1)
                fn(ah[:, 4 * g:4 * g + 4].rearrange("p h d -> p (h d)"), bank[:, 4 + g % 2], ACT.Copy
                   ).then_inc(ah_made, 1)

            fold_hi(0)
            fold_hi(1)
            act.wait_ge(fnmax_made, 1)
            fn(fexp[:], bank[0:B * FH, 0, 0:M], ACT.Exp, bias=fnmax[:, 0:1], accum_out=fsum[:, 0:1]
               ).then_inc(fexp_made, 1)
            act.wait_ge(d_ln, 16)

            def context_gain(c):
                act.wait_ge(ctxT_made, c + 1)
                fn(kv[:, :, c * P:(c + 1) * P], bank[:, 6 + c].rearrange("p (b j) -> p b j", b=B),
                   ACT.Identity, bias=ln_sb[:, 1:2], scale=ln_sb[:, 0:1]).then_inc(kv_made, 1)

            def latent_gain(b):
                act.wait_ge(latT_made, b + 1)
                fn(kv[:, b, S:J], bank[:, TB_B if b == 0 else V_B, 0:S], ACT.Identity,
                   bias=ln_sb[:, 3:4], scale=ln_sb[:, 2:3]).then_inc(kv_made, 1)

            context_gain(0)
            act.wait_ge(d_wv, 16)
            fn(wvh[:], wv_sb[:], ACT.Copy).then_inc(wvh_made, 1)
            context_gain(1)
            act.wait_ge(g_made, 1)
            fn(g_sb, bank[:, 1], ACT.Copy).then_inc(g_copied, 1)
            fold_hi(2)
            fold_hi(3)

            def values_hi(g):
                b, jt, half = V_GROUPS[g]
                act.wait_ge(v_made, g + 1)
                if b >= 2:
                    act.wait_ge(o_made, H * (b - 1))
                fn(vt[:, b % 2, jt, 8 * half:8 * half + 8, 0:DH],
                   bank[:, v_bank(g)].rearrange("p (h d) -> p h d", h=8), ACT.Copy, scale=V_SCALE
                   ).then_inc(vh_made, 1)

            for g in range(V_EARLY):
                values_hi(g)
            latent_gain(0)

            def t_hi(n):
                act.wait_ge(t_made, n + 1)
                if n >= 4:
                    act.wait_ge(s_made, 2 * (n - 3))
                fn(th[:, n % 4], bank[:, TB_B, 0:S], ACT.Copy, scale=SCALE
                   ).then_inc(th_made, 1)

            t_hi(0)
            t_hi(1)
            def exponent(n, c):
                u = 2 * n + c
                act.wait_ge(max_made, u + 1)
                if n >= 2:
                    act.wait_ge(pT_made, u - 3)
                fn(pr[:, u % 4], bank[:, S_B + c], ACT.Exp, bias=nmax[:, u:u + 1],
                   accum_out=psm[:, u:u + 1]).then_inc(exp_made, 1)

            def probs_hi(n, c):
                act.wait_ge(pT_made, 2 * n + c + 1)
                if n >= 2:
                    act.wait_ge(o_made, n - 1)
                fn(pth[:, n % 2, c].rearrange("p a q -> p (a q)"), bank[:, T_B + c], ACT.Copy,
                   scale=P_SCALE).then_inc(pth_made, 1)

            def out_copy(n):
                act.wait_ge(o_made, n + 1)
                if n >= 3:
                    act.wait_ge(y_part, n - 2)
                fn(oT[:, n % 3], bank[:, O_B, 0:S], ACT.Copy,
                   scale=1.0 / (P_SCALE * V_SCALE)).then_inc(o_sb, 1)

            def x2T_copy(b):
                act.wait_ge(x2T_made, b + 1)
                fn(xT[:, b], bank[:, V_B, 0:S], ACT.Copy).then_inc(xT_made, 1)

            def gate_exp(i):
                act.wait_ge(top_made, i + 1)
                ks = G_TILES[i]
                fn(ge2[:, ks], top[:, ks, 0:2], ACT.Exp, scale=-1.0).then_inc(ge_made, 1)

            for u in range(2 * STEPS):
                n, c = u // 2, u % 2
                if 0 <= u - 3 < 2 * NH:
                    probs_hi((u - 3) // 2, (u - 3) % 2)
                if n < NH:
                    exponent(n, c)
                if c == 0 and n + 2 < NH:
                    t_hi(n + 2)
                if c == 1 and 2 <= n < NH + 2:
                    out_copy(n - 2)
                for g in v_at.get(u, []):
                    values_hi(g)
                for b in range(B):
                    if b and u == lat_at(b, "turn"):
                        latent_gain(b)
                    if b < LAST_NORM and u == x2_at(b, "turn"):
                        x2T_copy(b)
                if u == ROUTE_AT + 2:
                    gate_exp(0)
            for m in range(2 * E):
                if m == 2:
                    x2T_copy(B - 1)
                if m == 4:
                    gate_exp(1)
                for k in range(FC):
                    i = 2 * m + k
                    act.wait_ge(gu_made, 4 * m + 2 * k + 1)
                    if i >= 2:
                        act.wait_ge(h_made, i - 1)
                    fn(sg[:, i % 2], bank[:, GU_B[2 * k]], ACT.Silu).then_inc(sg_made, 1)

        @block.gpsimd
        def _(pool):
            pool.wait_ge(d_fr, 16)
            nc.gpsimd.tensor_tensor(fqk[:], fr_sb[:, 0], fr_sb[:, 1], ALU.mult).then_inc(fqk_made, 1)

            rstds = [0]

            def rstd(i, tiles):
                rstds[0] += 1
                pool.wait_ge(ve_made, rstds[0])
                nc.gpsimd.tensor_tensor(rs[:, i, tiles], ve[:, i, tiles],
                                        cst[:, HALF0:HALF0 + 8][:, tiles], ALU.pow).then_inc(rs_made, 1)

            pool.wait_ge(d_cst, 16)
            rstd(0, slice(0, 8))

            def split_context(c):
                pool.wait_ge(kvh_made, c + 1)
                at = (slice(None), slice(None), slice(c * P, c * P + P))
                nc.gpsimd.tensor_tensor(kvl[at], kv[at], kvh[at], ALU.subtract).then_inc(kvl_made, 1)

            pool.wait_ge(wvh_made, 1)
            nc.gpsimd.tensor_tensor(wvl[:], wv_sb[:], wvh[:], ALU.subtract).then_inc(wvl_made, 1)
            for c in range(C):
                split_context(c)
            for i in (1, 2):
                rstd(i, slice(0, 8, B))

            def normalise(n, c):
                u = 2 * n + c
                pool.wait_ge(rcp_made, u + 1)
                nc.gpsimd.tensor_tensor(pr[:, u % 4], pr[:, u % 4],
                                        rcp[:, u:u + 1].to_broadcast([P, J]), ALU.mult
                                        ).then_inc(pn_made, 1)

            for u in range(2 * STEPS):
                n = u // 2
                if n < NH:
                    normalise(n, u % 2)
                if 5 <= n < 5 + 2 * E and u % 4 == 3:
                    e = (n - 5) // 2
                    pool.wait_ge(wgh_made, e + 1)
                    nc.gpsimd.tensor_tensor(wgl[:, e], wraw[:, e % 2], wgh[:, e], ALU.subtract
                                            ).then_inc(wgl_made, 1)
                for b in range(1, B):
                    if u == lat_at(b, "var"):
                        rstd(1, slice(b, 8, B))
                    if u == lat_at(b, "var2"):
                        rstd(2, slice(b, 8, B))
                for b in range(LAST_NORM):
                    if u == x2_at(b, "var"):
                        rstd(3, slice(b, 8, B))
                    if u == x2_at(b, "split"):
                        pool.wait_ge(xTh_made, b + 1)
                        nc.gpsimd.tensor_tensor(xTl[:, b], xT[:, b], xTh[:, b], ALU.subtract
                                                ).then_inc(xTl_made, 1)
            b = B - 1
            rstd(3, slice(b, 8, B))
            pool.wait_ge(xTh_made, b + 1)
            nc.gpsimd.tensor_tensor(xTl[:, b], xT[:, b], xTh[:, b], ALU.subtract).then_inc(xTl_made, 1)
            for hf in range(2):
                for c in range(C):
                    rstd(4, slice(c * B + 2 * hf, c * B + 2 * hf + 2))

        @block.vector
        def _(dve):
            v = nc.vector
            own = [0]

            def mark(ins):
                own[0] += 1
                ins.then_inc(dve_own, 1)

            def settle():
                dve.wait_ge(dve_own, own[0])

            def tile_stats(i, src, tiles):
                for k in tiles:
                    mark(v.bn_stats(st[:, i, k], src[:, k // B, k % B]))

            def variances(i, tiles):
                settle()
                for k in tiles:
                    mark(v.bn_aggr(mv[:, i, k], st[:, i, k]))
                settle()
                ks = slice(tiles[0], 8, tiles[1] - tiles[0])
                v.tensor_scalar(ve[:, i, ks], mv[:, i, ks, 1], EPS, None, ALU.add).then_inc(ve_made, 1)

            def statistics(i, src, tiles):
                tile_stats(i, src, tiles)
                variances(i, tiles)

            rstds = [0]

            def await_rstd():
                rstds[0] += 1
                dve.wait_ge(rs_made, rstds[0])

            def centre(i, dst, src, k):
                return v.tensor_scalar(dst[:, k // B, k % B], src[:, k // B, k % B], mv[:, i, k, 0:1],
                                       rs[:, i, k:k + 1], ALU.subtract, ALU.mult)

            every = list(range(8))
            dve.wait_ge(d_ctx, 32)
            statistics(0, ct, every)
            await_rstd()
            for k in every[:B]:
                last = centre(0, ct, ct, k)
            last.then_inc(zc_made, 1)
            both = [P, 2 * B, M]
            dve.wait_ge(qkv_made, 1)
            dve.wait_ge(fqk_made, 1)
            mark(v.tensor_tensor(qw, bank[:, 1].rearrange("p (a m) -> p a m", m=M),
                                 fqk[:].unsqueeze(1).to_broadcast(both), ALU.mult))
            dve.wait_ge(qkv_made, 2)
            settle()
            v.tensor_tensor(qk, bank[:, 2].rearrange("p (a m) -> p a m", m=M), qw, ALU.mult
                            ).then_inc(qk_sb, 1)
            dve.wait_ge(qkv_made, 3)
            dve.wait_ge(d_fr, 16)
            mark(v.tensor_tensor(vw.rearrange("p b a m -> p (b a) m"),
                                 bank[:, 3].rearrange("p (a m) -> p a m", m=M),
                                 fr_sb[:, 2].unsqueeze(1).to_broadcast(both), ALU.mult))
            dve.wait_ge(fs_made, 1)
            v.tensor_reduce(fnmax[:, 0:1], bank[0:B * FH, 0, 0:M], AX_X, ALU.max, negate=True
                            ).then_inc(fnmax_made, 1)
            for k in every[B:]:
                last = centre(0, ct, ct, k)
            last.then_inc(zc_made, 1)

            def fold_lo(g):
                dve.wait_ge(ah_made, g + 1)
                v.tensor_tensor(al[:, 4 * g:4 * g + 4].rearrange("p h d -> p (h d)"), bank[:, 4 + g % 2],
                                ah[:, 4 * g:4 * g + 4].rearrange("p h d -> p (h d)"), ALU.subtract
                                ).then_inc(al_made, 1)

            dve.wait_ge(fexp_made, 1)
            mark(v.reciprocal(frcp[:, 0:1], fsum[:, 0:1]))
            settle()
            v.tensor_scalar(fattn[:], fexp[:], frcp[:, 0:1], None, ALU.mult).then_inc(fattn_sb, 1)
            fold_lo(0)
            dve.wait_ge(fab_made, 1)
            v.tensor_tensor(ot, vw,
                            bank[:, 0, 256:512].rearrange("p (b m) -> p b m", b=B).unsqueeze(2)
                            .to_broadcast([P, B, 2, M]), ALU.mult).then_inc(ot_sb, 1)
            fold_lo(1)
            for c in range(C):
                dve.wait_ge(kv_made, c + 1)
                v.tensor_copy(kvh[:, :, c * P:(c + 1) * P], kv[:, :, c * P:(c + 1) * P]
                              ).then_inc(kvh_made, 1)

            def split_latents(b):
                dve.wait_ge(kv_made, C + b + 1)
                v.tensor_copy(kvh[:, b, S:J], kv[:, b, S:J]).then_inc(kvh_made, 1)
                dve.wait_ge(kvh_made, C + b + 1)
                v.tensor_tensor(kvl[:, b, S:J], kv[:, b, S:J], kvh[:, b, S:J], ALU.subtract
                                ).then_inc(kvl_made, 1)

            def values_lo(g):
                b, jt, half = V_GROUPS[g]
                dve.wait_ge(vh_made, g + 1)
                heads = slice(8 * half, 8 * half + 8)
                v.scalar_tensor_tensor(out=vt[:, b % 2, jt, heads, DH:2 * DH],
                                       in0=bank[:, v_bank(g)].rearrange("p (h d) -> p h d", h=8),
                                       scalar=V_SCALE, in1=vt[:, b % 2, jt, heads, 0:DH],
                                       op0=ALU.mult, op1=ALU.subtract).then_inc(vl_made, 1)

            def first_norm_out(b):
                await_rstd()
                for k in (b, B + b):
                    mark(centre(1, x1, xt, k))

            def latents_out(b):
                await_rstd()
                for k in (b, B + b):
                    last = centre(2, zl, x1, k)
                last.then_inc(zl_made, 1)

            for c in range(C):
                dve.wait_ge(y1_made, c + 1)
                mark(v.tensor_tensor(xt[:, c].rearrange("p b d -> p (b d)"), bank[:, 2 + c],
                                     xt[:, c].rearrange("p b d -> p (b d)"), ALU.add))
            settle()
            statistics(1, xt, [0, B])
            fold_lo(2)
            first_norm_out(0)
            settle()
            statistics(2, x1, [0, B])
            fold_lo(3)
            latents_out(0)
            for g in range(V_EARLY):
                values_lo(g)
            split_latents(0)

            def t_lo(n):
                dve.wait_ge(th_made, n + 1)
                v.scalar_tensor_tensor(out=tl[:, n % 4], in0=bank[:, TB_B, 0:S],
                                       scalar=SCALE, in1=th[:, n % 4].bitcast(F32), op0=ALU.mult,
                                       op1=ALU.subtract).then_inc(tl_made, 1)

            t_lo(0)
            t_lo(1)
            def row_max(n, c):
                u = 2 * n + c
                dve.wait_ge(s_made, u + 1)
                v.tensor_reduce(nmax[:, u:u + 1], bank[:, S_B + c], AX_X, ALU.max, negate=True
                                ).then_inc(max_made, 1)

            def sum_reciprocal(n, c):
                u = 2 * n + c
                dve.wait_ge(exp_made, u + 1)
                v.reciprocal(rcp[:, u:u + 1], psm[:, u:u + 1]).then_inc(rcp_made, 1)

            def probs_lo(n, c):
                dve.wait_ge(pth_made, 2 * n + c + 1)
                v.scalar_tensor_tensor(out=ptl[:, n % 2, c].rearrange("p a q -> p (a q)"),
                                       in0=bank[:, T_B + c], scalar=P_SCALE,
                                       in1=pth[:, n % 2, c].rearrange("p a q -> p (a q)"),
                                       op0=ALU.mult, op1=ALU.subtract).then_inc(ptl_made, 1)

            def second_norm_in(b):
                dve.wait_ge(y_part, H * (b + 1))
                ins = v.tensor_tensor(acc[:, :, b], bank[:, Y_B, 0:C * D].rearrange(
                    "p (c d) -> p c d", c=C), x1[:, :, b], ALU.add)
                ins.then_inc(y_used, 1)

            def second_norm_out(b):
                await_rstd()
                for c in range(C):
                    last = centre(3, x2, acc, c * B + b)
                last.then_inc(x2_made, 1)

            def split_x2T(b):
                dve.wait_ge(xT_made, b + 1)
                v.tensor_copy(xTh[:, b], xT[:, b]).then_inc(xTh_made, 1)

            def top_two(i):
                ks = G_TILES[i]
                tiles = range(ks.start, ks.stop)
                dve.wait_ge(lg_made, i + 1)
                v.tensor_copy(lg[:, ks], bank[:, V_B, ks.start * E:ks.stop * E].rearrange(
                    "p (k e) -> p k e", e=E)).then_inc(lg_copied, 1)
                dve.wait_ge(lg_copied, i + 1)
                for k in tiles:
                    mark(v.max(top[:, k], lg[:, k]))
                settle()
                for k in tiles:
                    mark(v.max_index(topi[:, k], top[:, k], lg[:, k]))
                settle()
                v.tensor_copy(topf[:, ks], topi[:, ks]).then_inc(top_made, 1)

            def make_gates(i):
                ks = G_TILES[i]
                wide = [P, ks.stop - ks.start, E]
                iota = cst[:, IO0:IO0 + 64].rearrange("p (k e) -> p k e", e=E)[:, ks]
                dve.wait_ge(top_made, i + 1)
                mark(v.tensor_tensor(m0[:, ks], iota, topf[:, ks, 0:1].to_broadcast(wide), ALU.is_equal))
                mark(v.tensor_tensor(m1[:, ks], iota, topf[:, ks, 1:2].to_broadcast(wide), ALU.is_equal))
                dve.wait_ge(ge_made, i + 1)
                mark(v.tensor_scalar(gn[:, ks], ge2[:, ks], 1.0, None, ALU.add))
                settle()
                mark(v.reciprocal(ge2[:, ks], gn[:, ks]))
                settle()
                mark(v.tensor_tensor(gs[:, ks], ge2[:, ks, 0], ge2[:, ks, 1], ALU.add))
                settle()
                mark(v.tensor_scalar(gs[:, ks], gs[:, ks], 1e-10, None, ALU.add))
                settle()
                mark(v.reciprocal(gr[:, ks], gs[:, ks]))
                settle()
                mark(v.tensor_tensor(gn[:, ks], ge2[:, ks],
                                     gr[:, ks].unsqueeze(2).to_broadcast([P, wide[1], 2]), ALU.mult))
                settle()
                mark(v.tensor_tensor(m0[:, ks], m0[:, ks], gn[:, ks, 0:1].to_broadcast(wide), ALU.mult))
                mark(v.tensor_tensor(m1[:, ks], m1[:, ks], gn[:, ks, 1:2].to_broadcast(wide), ALU.mult))
                settle()
                mark(v.tensor_tensor(gate[:, ks], m0[:, ks], m1[:, ks], ALU.add))

            for u in range(2 * STEPS):
                n, c = u // 2, u % 2
                if n < NH:
                    row_max(n, c)
                if 0 <= u - 3 < 2 * NH:
                    probs_lo((u - 3) // 2, (u - 3) % 2)
                if 0 <= u - 1 < 2 * NH:
                    sum_reciprocal((u - 1) // 2, (u - 1) % 2)
                for g in v_at.get(u - 1, []):
                    values_lo(g)
                if c == 1 and n + 2 < NH:
                    t_lo(n + 2)
                if 4 <= n < 4 + 2 * E and n % 2 == 0 and c == 0:
                    e = (n - 4) // 2
                    dve.wait_ge(d_raw[e % 2], 16 * (e // 2 + 1))
                    v.tensor_copy(wgh[:, e], wraw[:, e % 2]).then_inc(wgh_made, 1)
                for b in range(1, B):
                    mine = [b, B + b]
                    if u == lat_at(b, "stats"):
                        tile_stats(1, xt, mine)
                    if u == lat_at(b, "var"):
                        variances(1, mine)
                    if u == lat_at(b, "norm1"):
                        first_norm_out(b)
                    if u == lat_at(b, "stats2"):
                        settle()
                        tile_stats(2, x1, mine)
                    if u == lat_at(b, "var2"):
                        variances(2, mine)
                    if u == lat_at(b, "norm2"):
                        latents_out(b)
                    if u == lat_at(b, "split"):
                        split_latents(b)
                for b in range(LAST_NORM):
                    mine = [b, B + b]
                    if u == x2_at(b, "add"):
                        second_norm_in(b)
                    if u == x2_at(b, "stats"):
                        dve.wait_ge(y_used, b + 1)
                        tile_stats(3, acc, mine)
                    if u == x2_at(b, "var"):
                        variances(3, mine)
                    if u == x2_at(b, "norm"):
                        second_norm_out(b)
                    if u == x2_at(b, "split"):
                        split_x2T(b)
                if u == ROUTE_AT + 1:
                    top_two(0)
                if u == ROUTE_AT + 3:
                    make_gates(0)
            def hidden(m):
                for k in range(FC):
                    i = 2 * m + k
                    dve.wait_ge(sg_made, i + 1)
                    dve.wait_ge(gu_made, 4 * m + 2 * k + 2)
                    if m >= 2:
                        dve.wait_ge(dn_made, m - 1)
                    v.tensor_tensor(hT[:, m % 2, k], bank[:, GU_B[2 * k + 1]], sg[:, i % 2], ALU.mult
                                    ).then_inc(h_made, 1)

            def accumulate(m):
                hf, e = m // E, m % E
                dve.wait_ge(dn_made, m + 1)
                settle()
                for t in range(4):
                    b, c = 2 * hf + t // C, t % C
                    last = v.scalar_tensor_tensor(out=acc[:, c, b], in0=bank[:, DN_B[m % 2], t * D:(t + 1) * D],
                                                  scalar=gate[:, C * b + c, e:e + 1],
                                                  in1=(x2 if e == 0 else acc)[:, c, b],
                                                  op0=ALU.mult, op1=ALU.add)
                    mark(last) if t < 3 else last.then_inc(dn_used, 1)
                dve.wait_ge(dn_used, m + 1)

            def last_norm(hf):
                settle()
                tiles = [c * B + 2 * hf + i for c in range(C) for i in range(2)]
                for k in tiles:
                    mark(v.bn_stats(st[:, 4, k], acc[:, k // B, k % B]))
                settle()
                for k in tiles:
                    mark(v.bn_aggr(mv[:, 4, k], st[:, 4, k]))
                settle()
                for c in range(C):
                    ks = slice(c * B + 2 * hf, c * B + 2 * hf + 2)
                    v.tensor_scalar(ve[:, 4, ks], mv[:, 4, ks, 1], EPS, None, ALU.add).then_inc(ve_made, 1)
                for c in range(C):
                    await_rstd()
                    for k in tiles[2 * c:2 * c + 2]:
                        centre(4, acc, acc, k).then_inc(fin_made, 1)

            hidden(0)
            second_norm_in(B - 1)
            dve.wait_ge(y_used, B)
            statistics(3, acc, [B - 1, 2 * B - 1])
            hidden(1)
            second_norm_out(B - 1)
            split_x2T(B - 1)
            top_two(1)
            for m in range(1, 2 * E):
                if m > 1:
                    hidden(m)
                accumulate(m - 1)
                if m == 4:
                    make_gates(1)
                if m - 1 == E - 1:
                    last_norm(0)
            accumulate(2 * E - 1)
            last_norm(1)


def constants():
    import numpy as np
    k = np.zeros((P, NCONST), np.float32)
    s, f = np.arange(S)[:, None], np.arange(M)[None, :]
    angle = 2 * np.pi * ((s * f) % S) / S
    cs = np.concatenate([np.cos(angle), np.sin(angle)], 1).astype(np.float32)
    for c in range(C):
        k[:, CS0 + c * P:CS0 + (c + 1) * P] = cs[c * P:(c + 1) * P]
    k[:, CST0:CST0 + S] = cs.T
    k[:, ID0:ID0 + P] = np.eye(P)
    for p in range(P):
        k[p, EB0 + 48 + p // HD] = 1
        for b in range(B):
            k[16 * b + p // HD, SEL0 + b * P + p] = 1
    k[:, IO0:IO0 + 64] = np.tile(np.arange(E), 8)
    k[:, HALF0:HALF0 + 8] = -0.5
    k[:, LEN0:LEN0 + B] = S
    return k


def kernel(**inputs):
    import numpy as np
    import concourse.bacc as bacc
    from concourse.bass_utils import run_bass_kernel_spmd

    a = {n: np.asarray(v) for n, v in inputs.items()}
    inner = H * DH
    wkv = a["L0_xattn_Wkv"]
    arrays = {
        "x": a["x"],
        "ctx_in": a["ctx_1024"],
        "w_qkvT": a["L0_attn_w_qkv"].T,
        "b_qkv": a["L0_attn_b_qkv"][None],
        "w_outT": a["L0_attn_w_out"].T,
        "b_out": a["L0_attn_b_out"][None],
        "freqT": np.concatenate([a[f"L0_attn_freq_{n}"].transpose(0, 2, 1).reshape(D, M) for n in "qkv"], 1),
        "ln_par": np.stack([a[f"L0_xattn_ln_{n}"] for n in ("m_g", "m_b", "l_g", "l_b")], 1),
        "wqT": a["L0_xattn_Wq"].T,
        "wkT": wkv[:, :inner].T,
        "wv": wkv[:, inner:],
        "wout": a["L0_xattn_Wout"],
        "routerT": a["L0_ffn_router_w"].T,
        "w_gu": np.concatenate([a["L0_ffn_w_gate"], a["L0_ffn_w_up"]], 2).transpose(1, 0, 2),
        "w_down": a["L0_ffn_w_down"],
        "consts": constants(),
    }
    arrays = {n: np.ascontiguousarray(v) for n, v in arrays.items()}
    nc = bacc.Bacc("TRN2", target_bir_lowering=False, num_devices=1)
    args = [nc.dram_tensor(f"in_{n}", v.shape, mybir.dt.from_np(v.dtype), kind="ExternalInput").ap()
            for n, v in arrays.items()]
    out = nc.dram_tensor("out", (B, S, D), F32, kind="ExternalOutput").ap()
    decoder_layer(nc, *args, out)
    r = run_bass_kernel_spmd(nc, [{f"in_{n}": v for n, v in arrays.items()}], core_ids=[0])
    return r.results[0]["out"]
```

```python
from contextlib import ExitStack

import concourse.bass as bass
from concourse import mybir

F32 = mybir.dt.float32
F32R = mybir.dt.float32r
F16 = mybir.dt.float16
U32 = mybir.dt.uint32
ALU = mybir.AluOpType
ACT = mybir.ActivationFunctionType
AX_X = mybir.AxisListType.X

P = 128
D = 128
B = 4
S = 256
C = S // P
M = 64
FH = 16
HD = D // FH
H = 16
DH = 64
J = 2 * S
JT = J // P
NH = B * H
E = 8
F = 256
FC = F // P
EPS = 1e-5
SCALE = DH ** -0.5
P_SCALE = 1024.0
V_SCALE = 64.0
H_SCALE = 16.0
W_SCALE = 64.0

CS0, CST0, ID0, EB0, SEL0, IO0, HALF0, LEN0, WS0, NCONST = (
    0, 256, 512, 640, 752, 1264, 1328, 1336, 1340, 1341)


def decoder_layer(nc, x, ctx_in, w_qkvT, b_qkv, w_outT, b_out, freqT, ln_par, wqT, wkT, wv, wout,
                  routerT, w_gu, w_down, consts, out):
    with ExitStack() as ctx:
        def sb(name, shape, dt=F32):
            return ctx.enter_context(nc.sbuf_tensor(name, shape, dt))

        def sem(name):
            return ctx.enter_context(nc.semaphore(name))

        cst = sb("cst", [P, NCONST])
        xt = sb("xt", [P, C, B, D])
        ct = sb("ct", [P, C, B, D])
        x1 = sb("x1", [P, C, B, D])
        zl = sb("zl", [P, C, B, D])
        x2 = zl
        acc = xt
        wqkv_sb = sb("wqkv_sb", [P, 3 * D])
        bqkv_sb = sb("bqkv_sb", [1, 3 * D])
        wo_sb = sb("wo_sb", [P, D])
        bo_sb = sb("bo_sb", [1, D])
        fr_sb = sb("fr_sb", [P, 3, M])
        ln_sb = sb("ln_sb", [P, 4])
        wqk_sb = sb("wqk_sb", [P, 2, H // 2, D])
        wqT_sb, wkT_sb = wqk_sb[:, 0], wqk_sb[:, 1]
        wv_sb = sb("wv_sb", [P, H * DH])
        wvh = sb("wvh", [P, H * DH], F32R)
        wvl = sb("wvl", [P, H * DH], F32R)
        wo2 = sb("wo2", [P, H // 2, D])
        rt_sb = sb("rt_sb", [P, E])
        work = sb("work", [P, 6, 512])
        ft = work[:, 0]
        fqk = sb("fqk", [P, M])
        qw = work[:, 1].rearrange("p (k m) -> p k m", m=M)
        qk = work[:, 2].rearrange("p (k m) -> p k m", m=M)
        vw = work[:, 3].rearrange("p (b a m) -> p b a m", b=B, a=2)
        ot = work[:, 4].rearrange("p (b a m) -> p b a m", b=B, a=2)
        fnmax = sb("fnmax", [B * FH, 1])
        fexp = sb("fexp", [B * FH, M])
        fsum = sb("fsum", [B * FH, 1])
        frcp = sb("frcp", [B * FH, 1])
        fattn = sb("fattn", [B * FH, M])
        g_sb = work[:, 5]
        st = sb("st", [P, 5, C * B, 6])
        mv = sb("mv", [P, 5, C * B, 2])
        ve = sb("ve", [P, 5, C * B])
        rs = sb("rs", [P, 5, C * B])
        ah = sb("ah", [P, H, D], F32R)
        al = sb("al", [P, H, D], F32R)
        kv = sb("kv", [P, B, J])
        kvh = sb("kvh", [P, B, J], F32R)
        kvl = sb("kvl", [P, B, J], F32R)
        th = sb("th", [P, 4, S], F32R)
        tl = sb("tl", [P, 4, S], F32R)
        traw = sb("traw", [P, 2, S])
        vraw = sb("vraw", [P, 2, 512])
        vt = sb("vt", [P, 2, JT, H, 2 * DH], F16)
        pr = wqk_sb[:].rearrange("p a k d -> p (a k d)").rearrange("p (i j) -> p i j", i=4)
        nmax = sb("nmax", [P, 2 * NH])
        psm = sb("psm", [P, 2 * NH])
        rcp = sb("rcp", [P, 2 * NH])
        pth = sb("pth", [P, 2, C, JT, P], F16)
        ptl = sb("ptl", [P, 2, C, JT, P], F16)
        on = sb("on", [P, 2, C, 2, DH])
        oT = sb("oT", [P, 2, S])
        wraw = ct[:].rearrange("p c b d -> p c (b d)")
        wgh = sb("wgh", [P, E, 2 * F], F32R)
        wgl = sb("wgl", [P, E, 2 * F], F32R)
        wd = kv[:].rearrange("p b j -> p (b j)")
        wdh = ct[:].rearrange("p c b d -> p (c b d)").bitcast(F16)
        wdl = work[:, 4:6].rearrange("p i t -> p (i t)").bitcast(F16)
        xT = wv_sb[:].rearrange("p (b s) -> p b s", b=B)
        xTh = sb("xTh", [P, B, S], F32R)
        xTl = sb("xTl", [P, B, S], F32R)
        lg = sb("lg", [P, 8, E])
        top = sb("top", [P, 8, 8])
        topi = sb("topi", [P, 8, 8], U32)
        topf = sb("topf", [P, 8, 8])
        ge2 = sb("ge2", [P, 8, 2])
        gs = sb("gs", [P, 8])
        gr = sb("gr", [P, 8])
        gn = sb("gn", [P, 8, 2])
        m0 = sb("m0", [P, 8, E])
        m1 = sb("m1", [P, 8, E])
        gate = sb("gate", [P, 8, E])
        sg = work[:, 0:2]
        hT = work[:, 2:4]
        hh = pth[:].rearrange("p i c a q -> p i c (a q)")
        hl = ptl[:].rearrange("p i c a q -> p i c (a q)")

        bank = ctx.enter_context(nc.psum_tensor("bank", [P, 8, 512], F32))
        S_B, T_B, O_B, TB_B, V_B, Y_B = 0, 2, 4, 5, 6, 7
        GU_B = (0, 1, 2, 3)
        DN_B = (5, 6)

        ident = cst[:, ID0:ID0 + P]
        one = cst[:, CS0:CS0 + 1]

        (d_x, d_cs, d_cst, d_ctx, d_wqkv, d_bq, d_fr, d_wo, d_ln, d_wq, d_wk, d_wv, d_wo2, d_rt,
         d_wd, d_out) = [sem(n) for n in (
            "d_x", "d_cs", "d_cst", "d_ctx", "d_wqkv", "d_bq", "d_fr", "d_wo", "d_ln", "d_wq", "d_wk",
            "d_wv", "d_wo2", "d_rt", "d_wd", "d_out")]
        d_raw = [sem("d_raw0"), sem("d_raw1")]
        ft_made, ft_sb, qkv_made, fqk_made, qk_sb, vw_sb, fs_made, fnmax_made, fexp_made = [
            sem(n) for n in ("ft_made", "ft_sb", "qkv_made", "fqk_made", "qk_sb", "vw_sb",
                             "fs_made", "fnmax_made", "fexp_made")]
        fattn_sb, fab_made, ot_sb, g_made, g_copied, y1_made, a_made, ah_made, al_made = [
            sem(n) for n in ("fattn_sb", "fab_made", "ot_sb", "g_made", "g_copied", "y1_made",
                             "a_made", "ah_made", "al_made")]
        zc_made, ctxT_made, kv_made, kvh_made, kvl_made, zl_made, latT_made = [
            sem(n) for n in ("zc_made", "ctxT_made", "kv_made", "kvh_made", "kvl_made", "zl_made",
                             "latT_made")]
        wvh_made, wvl_made, v_made, vh_made, vl_made, t_made, th_made, tl_made = [
            sem(n) for n in ("wvh_made", "wvl_made", "v_made", "vh_made", "vl_made", "t_made",
                             "th_made", "tl_made")]
        s_made, max_made, exp_made, rcp_made, pT_made, pth_made, ptl_made = [
            sem(n) for n in ("s_made", "max_made", "exp_made", "rcp_made", "pT_made",
                             "pth_made", "ptl_made")]
        oT_made, oT_sb = sem("oT_made"), sem("oT_sb")
        t_copied, v_copied, vp_made = sem("t_copied"), sem("v_copied"), sem("vp_made")
        o_made, o_sb, y_part, y_used, x2_made, x2T_made, xT_made, xTh_made, xTl_made = [
            sem(n) for n in ("o_made", "o_sb", "y_part", "y_used", "x2_made", "x2T_made",
                             "xT_made", "xTh_made", "xTl_made")]
        ve_made, rs_made, wgh_made, wgl_made = [
            sem(n) for n in ("ve_made", "rs_made", "wgh_made", "wgl_made")]
        lg_made, lg_copied, top_made, ge_made, gate_made = [
            sem(n) for n in ("lg_made", "lg_copied", "top_made", "ge_made", "gate_made")]
        gu_made, sg_made, h_made, dn_made, dn_used, fin_made = [
            sem(n) for n in ("gu_made", "sg_made", "h_made", "dn_made", "dn_used", "fin_made")]
        wds_made, wdh_made, wdl_made, hh_made, hl0_made, hl1_made = [
            sem(n) for n in ("wds_made", "wdh_made", "wdl_made", "hh_made", "hl0_made", "hl1_made")]
        dve_own = sem("dve_own")

        STEPS = NH + 4

        def fold_slot(h):
            return 4 * (2 * (h // 8) + h % 2) + h % 8 // 2

        V_GROUPS = [(b, jt, half) for b in range(B) for jt in range(JT) for half in range(2)]
        V_EARLY = 2 * C
        v_at = {}
        for g in range(V_EARLY, 8 * B):
            at = g - V_EARLY if g < 8 else 2 * (H * (g // 8 - 1) + 2 * (g % 8) + 1 + (g == 8)) + 1
            v_at.setdefault(at, []).append(g)

        G_TILES = (slice(0, C * (B - 1)), slice(C * (B - 1), C * B))

        def v_bank(g):
            return V_B + (g % 2 if g < 8 else 0)

        def v_left(pe, count):
            if count <= 8:
                pe.wait_ge(vl_made, count)
            else:
                pe.wait_ge(v_copied, count - 8)

        def v_before(u):
            return V_EARLY + sum(len(gs) for at, gs in v_at.items() if at < u)

        def lat_at(b, piece):
            return 2 * H * (b - 1) + dict(stats=0, var=1, norm1=5, stats2=6, var2=7, norm2=11,
                                          turn=13, split=15)[piece]

        def x2_at(b, piece):
            return 2 * H * (b + 1) + dict(add=7, stats=8, var=9, norm=13, turn=17, split=19)[piece]

        GU_EARLY = (2 * NH, 2 * NH + 1, 2 * NH + 3, 2 * NH + 4)
        WD_AT = [2 * H * (B - 1) + 2 + 4 * i for i in range(4)]
        ROUTE_AT = x2_at(B - 2, "turn") + 4
        LAST_NORM = B - 1

        block = ctx.enter_context(nc.Block())

        @block.sync
        def _(sp):
            for c in range(C):
                sp.dma_start(xt[:, c], x.rearrange("b (c p) d -> c p b d", p=P)[c]).then_inc(d_x, 16)
            sp.dma_start(wqkv_sb[:], w_qkvT).then_inc(d_wqkv, 16)
            sp.dma_start(bqkv_sb[:], b_qkv).then_inc(d_bq, 16)
            sp.dma_start(fr_sb[:], freqT.rearrange("p (a m) -> p a m", a=3)).then_inc(d_fr, 16)
            sp.dma_start(wqT_sb, wqT.rearrange("(k p) d -> p k d", p=P)).then_inc(d_wq, 16)
            sp.dma_start(wkT_sb, wkT.rearrange("(k p) d -> p k d", p=P)).then_inc(d_wk, 16)
            sp.dma_start(wo_sb[:], w_outT).then_inc(d_wo, 16)
            sp.dma_start(bo_sb[:], b_out).then_inc(d_wo, 16)
            sp.dma_start(wv_sb[:], wv).then_inc(d_wv, 16)
            sp.dma_start(wo2[:], wout.rearrange("(j p) n -> p j n", p=P)).then_inc(d_wo2, 16)
            sp.dma_start(rt_sb[:], routerT).then_inc(d_rt, 16)
            sp.wait_ge(ctxT_made, 2)
            for e in range(E):
                if e >= 2:
                    sp.wait_ge(wgl_made, e - 1)
                sp.dma_start(wraw[:, e % 2], w_gu[:, e]).then_inc(d_raw[e % 2], 16)
            sp.wait_ge(kvl_made, C + B)
            sp.wait_ge(kvh_made, C + B)
            sp.dma_start(wd.rearrange("p (e c n) -> p e c n", e=E, c=FC),
                         w_down.rearrange("e (c p) n -> p e c n", p=P)).then_inc(d_wd, 16)
            for b in range(B):
                sp.wait_ge(fin_made, C * (b + 1))
                sp.dma_start(out.rearrange("b (c p) d -> b p c d", p=P)[b], acc[:, :, b]
                             ).then_inc(d_out, 16)
            sp.wait_ge(d_out, 16 * B)

        @block.tensor
        def _(pe):
            mm = nc.tensor.matmul

            def three(dst, wh, wl, mh, ml):
                mm(dst, wh, mh, start=True, stop=False)
                mm(dst, wh, ml, start=False, stop=False)
                return mm(dst, wl, mh, start=False, stop=True)

            pe.wait_ge(d_x, 32)
            pe.wait_ge(d_cs, 16)
            for b in range(B):
                for c in range(C):
                    last = mm(bank[:, 0, b * P:(b + 1) * P], xt[:, c, b],
                              cst[:, CS0 + c * P:CS0 + (c + 1) * P], start=(c == 0), stop=(c == C - 1))
            last.then_inc(ft_made, 1)

            def fold_heads(g):
                pe.wait_ge(d_wq, 16)
                pe.wait_ge(d_wk, 16)
                if g >= 2:
                    pe.wait_ge(al_made, g - 1)
                q = slice(DH * (g % 2), DH * (g % 2) + DH)
                for i in range(4):
                    k = 4 * (g // 2) + i
                    last = mm(bank[:, 4 + g % 2, i * D:(i + 1) * D], wqT_sb[q, k], wkT_sb[q, k],
                              start=True, stop=True)
                last.then_inc(a_made, 1)

            pe.wait_ge(ft_sb, 1)
            pe.wait_ge(d_wqkv, 16)
            pe.wait_ge(d_bq, 16)
            pe.wait_ge(d_cst, 16)
            for i in range(3):
                mm(bank[:, 1 + i], wqkv_sb[:, i * D:(i + 1) * D], ft, start=True, stop=False)
                mm(bank[:, 1 + i].rearrange("p (b f) -> p b f", b=B)[:, :, 0],
                   bqkv_sb[0:1, i * D:(i + 1) * D], cst[0:1, LEN0:LEN0 + B], start=False, stop=True
                   ).then_inc(qkv_made, 1)
            pe.wait_ge(qk_sb, 1)
            for k in range(2 * B):
                b = k // 2
                last = mm(bank[0:B * FH, 0, 0:M], cst[:, EB0 + 48 - 16 * b:EB0 + 112 - 16 * b],
                          qk[:, k], start=(k == 0), stop=(k == 2 * B - 1))
            last.then_inc(fs_made, 1)
            fold_heads(0)

            def context_T(c):
                pe.wait_ge(zc_made, c + 1)
                for b in range(B):
                    last = nc.tensor.transpose(bank[:, 6 + c, b * P:(b + 1) * P], ct[:, c, b], ident)
                last.then_inc(ctxT_made, 1)

            context_T(0)
            fold_heads(1)
            pe.wait_ge(fattn_sb, 1)
            for b in range(B):
                last = mm(bank[:, 0, 256 + b * M:256 + (b + 1) * M],
                          cst[0:B * FH, SEL0 + b * P:SEL0 + (b + 1) * P], fattn[:], start=True, stop=True)
            last.then_inc(fab_made, 1)
            context_T(1)
            pe.wait_ge(ot_sb, 1)
            pe.wait_ge(d_wo, 32)
            for b in range(B):
                dst = bank[:, 0, 0:D] if b == 0 else bank[:, 1, b * D:(b + 1) * D]
                mm(dst, ot[:, b].rearrange("p a m -> p (a m)"), wo_sb[:], start=True, stop=False)
                last = mm(dst, ident[0:1, :], bo_sb[:], start=False, stop=True)
                if b in (0, B - 1):
                    last.then_inc(g_made, 1)
            pe.wait_ge(g_copied, 1)
            for c in range(C):
                last = mm(bank[:, 2, c * D:(c + 1) * D], cst[:, CST0 + c * P:CST0 + (c + 1) * P],
                          g_sb[:, 0:D], start=True, stop=True)
            last.then_inc(y1_made, 1)
            pe.wait_ge(g_copied, 2)
            for c in range(C):
                mm(bank[:, (3, 1)[c], D:B * D], cst[:, CST0 + c * P:CST0 + (c + 1) * P],
                   g_sb[:, D:B * D], start=True, stop=True).then_inc(y1_made, 1)
            fold_heads(2)
            fold_heads(3)

            def values(g):
                b, jt, half = V_GROUPS[g]
                if g >= 2:
                    v_left(pe, g - 1 if g <= 8 else g)
                cols = slice(half * 512, half * 512 + 512)
                keys = slice(jt * P, jt * P + P)
                three(bank[:, v_bank(g)], kvh[:, b, keys], kvl[:, b, keys], wvh[:, cols], wvl[:, cols]
                      ).then_inc(v_made, 1)

            def latents_T(b):
                pe.wait_ge(zl_made, b + 1)
                for c in range(C):
                    last = nc.tensor.transpose(bank[:, 0 if b == 0 else V_B, c * P:(c + 1) * P],
                                               zl[:, c, b], ident)
                last.then_inc(latT_made, 1)

            pe.wait_ge(wvl_made, 1)
            pe.wait_ge(kvl_made, 1)
            values(0)
            values(1)
            latents_T(0)
            pe.wait_ge(kvl_made, 2)
            values(2)

            def t_head(n):
                b, h = n // H, n % H
                if 1 <= n <= 2:
                    pe.wait_ge(tl_made, n)
                elif n >= 3:
                    pe.wait_ge(t_copied, n - 2)
                three(bank[:, TB_B, 0:S], ah[:, fold_slot(h)], al[:, fold_slot(h)], kvh[:, b, S:J], kvl[:, b, S:J]
                      ).then_inc(t_made, 1)

            pe.wait_ge(kvl_made, C + 1)
            pe.wait_ge(al_made, 4)
            t_head(0)
            values(3)
            t_head(1)

            def scores(n, c):
                if n >= 1:
                    pe.wait_ge(exp_made, 2 * (n - 1) + c + 1)
                b = n // H
                q = slice(c * P, c * P + P)
                three(bank[:, S_B + c], th[:, n % 4, q], tl[:, n % 4, q], kvh[:, b], kvl[:, b]
                      ).then_inc(s_made, 1)

            def transposes(n, c):
                pe.wait_ge(exp_made, 2 * n + c + 1)
                if n >= 1:
                    pe.wait_ge(ptl_made, 2 * (n - 1) + c + 1)
                for jt in range(JT):
                    last = nc.tensor.transpose(bank[:, T_B + c, jt * P:(jt + 1) * P],
                                               pr[:, (2 * n + c) % 4, jt * P:(jt + 1) * P], ident)
                last.then_inc(pT_made, 1)

            def attend(n):
                b, h = n // H, n % H
                pe.wait_ge(ptl_made, 2 * n + 2)
                if b == 0:
                    pe.wait_ge(vl_made, 8)
                else:
                    pe.wait_ge(vp_made, 8 * b)
                if n >= 1:
                    pe.wait_ge(o_sb, n)
                if n >= 3:
                    pe.wait_ge(oT_sb, (n - 1) // 2)
                for c in range(C):
                    dst = bank[:, O_B, c * DH:(c + 1) * DH]
                    for jt in range(JT):
                        ph, pl = pth[:, n % 2, c, jt], ptl[:, n % 2, c, jt]
                        vh, vl = vt[:, b % 2, jt, h, 0:DH], vt[:, b % 2, jt, h, DH:2 * DH]
                        mm(dst, ph, vh, start=(jt == 0), stop=False)
                        mm(dst, ph, vl, start=False, stop=False)
                        last = mm(dst, pl, vh, start=False, stop=(jt == JT - 1))
                last.then_inc(o_made, 1)

            def transpose_pair(j):
                pe.wait_ge(o_sb, 2 * j + 2)
                for c in range(C):
                    last = nc.tensor.transpose(bank[:, O_B, P + c * P:P + (c + 1) * P],
                                               on[:, j % 2, c].rearrange("p r d -> p (r d)"), ident)
                last.then_inc(oT_made, 1)

            def project(j):
                b, i = j // (H // 2), j % (H // 2)
                pe.wait_ge(oT_sb, j + 1)
                if j == 0:
                    pe.wait_ge(d_wo2, 16)
                    pe.wait_ge(vl_made, 8)
                if i == 0 and b >= 1:
                    pe.wait_ge(y_used, b)
                for c in range(C):
                    last = mm(bank[:, Y_B, c * D:(c + 1) * D], oT[:, j % 2, c * P:(c + 1) * P],
                              wo2[:, i], start=(i == 0 and c == 0), stop=(i == H // 2 - 1),
                              skip_group_check=True)
                last.then_inc(y_part, 1)

            def transpose_x2(b):
                pe.wait_ge(x2_made, b + 1)
                v_left(pe, v_before(x2_at(b, "turn")))
                for c in range(C):
                    last = nc.tensor.transpose(bank[:, V_B, c * P:(c + 1) * P], x2[:, c, b], ident)
                last.then_inc(x2T_made, 1)

            def router(tiles):
                pe.wait_ge(d_rt, 16)
                for b, c in tiles:
                    k = C * b + c
                    last = mm(bank[:, V_B, k * E:(k + 1) * E], xT[:, b, c * P:(c + 1) * P],
                              rt_sb[:], start=True, stop=True)
                last.then_inc(lg_made, 1)

            def gate_up(m, ks):
                hf, e = m // E, m % E
                for k in ks:
                    part = (0, 2, 1, 3)[k]
                    if m:
                        pe.wait_ge(h_made, 2 * (m - 1) + k // 2 + 1)
                    cols = slice(part * P, part * P + P)
                    w = slice(2 * hf, 2 * hf + 2)
                    three(bank[:, GU_B[k]], wgh[:, e, cols], wgl[:, e, cols],
                          xTh[:, w].rearrange("p b s -> p (b s)"),
                          xTl[:, w].rearrange("p b s -> p (b s)")).then_inc(gu_made, 1)

            for u in range(2 * STEPS):
                n, c = u // 2, u % 2
                if 0 <= u - 3 < 2 * NH:
                    transposes((u - 3) // 2, (u - 3) % 2)
                if u in GU_EARLY[:2]:
                    pe.wait_ge(xTl_made, 2)
                    pe.wait_ge(wgl_made, E)
                    pe.wait_ge(exp_made, u - 1)
                    gate_up(0, (u - GU_EARLY[0],))
                if u == GU_EARLY[2]:
                    pe.wait_ge(ptl_made, 2 * NH - 1)
                    gate_up(0, (2,))
                if n < NH:
                    pe.wait_ge(tl_made, n + 1)
                    if n % H == 0:
                        pe.wait_ge(kvl_made, C + n // H + 1)
                    scores(n, c)
                if c == 0 and n % 2 == 1 and n >= 5:
                    project((n - 5) // 2)
                if c == 0 and n + 2 < NH:
                    if (n + 2) % H == 0:
                        pe.wait_ge(kvl_made, C + (n + 2) // H + 1)
                    t_head(n + 2)
                if c == 1 and 2 <= n < NH + 2:
                    attend(n - 2)
                if c == 1 and n % 2 == 0 and 4 <= n < NH + 4:
                    transpose_pair((n - 4) // 2)
                for g in v_at.get(u, []):
                    b, jt, half = V_GROUPS[g]
                    if jt >= C:
                        pe.wait_ge(kvl_made, C + b + 1)
                    for k in range(B):
                        if k < B - 1 and u - 2 == x2_at(k, "turn"):
                            pe.wait_ge(xT_made, k + 1)
                        if k and u - 2 == lat_at(k, "turn"):
                            pe.wait_ge(kv_made, C + k + 1)
                    values(g)
                for b in range(B):
                    if b and u == lat_at(b, "turn"):
                        v_left(pe, v_before(u))
                        latents_T(b)
                    if b < LAST_NORM and u == x2_at(b, "turn"):
                        transpose_x2(b)
                if u == ROUTE_AT:
                    pe.wait_ge(xT_made, LAST_NORM)
                    v_left(pe, 8 * B)
                    router([(b, c) for b in range(LAST_NORM) for c in range(C)])
                if u == GU_EARLY[3]:
                    pe.wait_ge(ptl_made, 2 * NH)
                    gate_up(0, (3,))

            def down(m):
                e = m % E
                pe.wait_ge(hh_made, 2 * m + 2)
                pe.wait_ge(hl0_made, m + 1)
                pe.wait_ge(hl1_made, m + 1)
                if m >= 2:
                    pe.wait_ge(dn_used, m - 1)
                for t in range(4):
                    dst = bank[:, DN_B[m % 2], t * D:(t + 1) * D]
                    for k in range(FC):
                        high, low = [part[:, m % 2, k, t * P:(t + 1) * P] for part in (hh, hl)]
                        w = slice((FC * e + k) * D, (FC * e + k + 1) * D)
                        mm(dst, high, wdh[:, w], start=(k == 0), stop=False)
                        mm(dst, high, wdl[:, w], start=False, stop=False)
                        last = mm(dst, low, wdh[:, w], start=False, stop=(k == FC - 1))
                last.then_inc(dn_made, 1)

            def last_down(m):
                e = m % E
                for k in range(FC):
                    pe.wait_ge(hh_made, 2 * m + k + 1)
                    pe.wait_ge((hl0_made, hl1_made)[k], m + 1)
                    for t in range(4):
                        dst = bank[:, GU_B[t // 2], t * D:(t + 1) * D]
                        high, low = [part[:, m % 2, k, t * P:(t + 1) * P] for part in (hh, hl)]
                        w = slice((FC * e + k) * D, (FC * e + k + 1) * D)
                        mm(dst, high, wdh[:, w], start=(k == 0 and t % 2 == 0), stop=False,
                           skip_group_check=True)
                        mm(dst, high, wdl[:, w], start=False, stop=False, skip_group_check=True)
                        last = mm(dst, low, wdh[:, w], start=False, stop=(k == FC - 1),
                                  skip_group_check=True)
                        if k == FC - 1 and t % 2 == 1:
                            last.then_inc(dn_made, 1)

            gate_up(1, range(4))
            pe.wait_ge(lg_copied, 1)
            transpose_x2(B - 1)
            pe.wait_ge(wdl_made, 4)
            pe.wait_ge(t_copied, NH - 2)
            down(0)
            pe.wait_ge(xT_made, B)
            router([(B - 1, c) for c in range(C)])
            gate_up(2, range(4))
            pe.wait_ge(lg_copied, 2)
            down(1)
            for m in range(3, 2 * E - 1):
                if m == E:
                    pe.wait_ge(xTl_made, B)
                gate_up(m, range(4))
                if m < 2 * E - 2:
                    down(m - 1)
            gate_up(2 * E - 1, range(4))
            down(2 * E - 3)
            down(2 * E - 2)
            last_down(2 * E - 1)

        @block.scalar
        def _(act):
            fn = nc.scalar.activation
            act.dma_start(cst[:, 0:256], consts[:, 0:256]).then_inc(d_cs, 16)
            for c in range(C):
                act.dma_start(ct[:, c], ctx_in.rearrange("b (c p) d -> c p b d", p=P)[c]).then_inc(d_ctx, 16)
            act.dma_start(cst[:, 256:], consts[:, 256:]).then_inc(d_cst, 16)
            act.dma_start(ln_sb[:], ln_par).then_inc(d_ln, 16)
            act.wait_ge(ft_made, 1)
            fn(ft, bank[:, 0], ACT.Copy).then_inc(ft_sb, 1)
            act.wait_ge(d_wv, 16)
            fn(wvh[:], wv_sb[:], ACT.Copy).then_inc(wvh_made, 1)

            def fold_hi(g):
                act.wait_ge(a_made, g + 1)
                fn(ah[:, 4 * g:4 * g + 4].rearrange("p h d -> p (h d)"), bank[:, 4 + g % 2], ACT.Copy
                   ).then_inc(ah_made, 1)

            act.wait_ge(fnmax_made, 1)
            fn(fexp[:], bank[0:B * FH, 0, 0:M], ACT.Exp, bias=fnmax[:, 0:1], accum_out=fsum[:, 0:1]
               ).then_inc(fexp_made, 1)
            fold_hi(0)
            act.wait_ge(d_ln, 16)

            def context_gain(c):
                act.wait_ge(ctxT_made, c + 1)
                fn(kv[:, :, c * P:(c + 1) * P], bank[:, 6 + c].rearrange("p (b j) -> p b j", b=B),
                   ACT.Identity, bias=ln_sb[:, 1:2], scale=ln_sb[:, 0:1]).then_inc(kv_made, 1)

            def latent_gain(b):
                act.wait_ge(latT_made, b + 1)
                fn(kv[:, b, S:J], bank[:, 0 if b == 0 else V_B, 0:S], ACT.Identity,
                   bias=ln_sb[:, 3:4], scale=ln_sb[:, 2:3]).then_inc(kv_made, 1)

            context_gain(0)
            fold_hi(1)
            context_gain(1)
            act.wait_ge(g_made, 1)
            fn(g_sb[:, 0:D], bank[:, 0, 0:D], ACT.Copy).then_inc(g_copied, 1)
            act.wait_ge(g_made, 2)
            fn(g_sb[:, D:B * D], bank[:, 1, D:B * D], ACT.Copy).then_inc(g_copied, 1)
            fold_hi(2)
            fold_hi(3)

            def values_hi(g):
                b, jt, half = V_GROUPS[g]
                act.wait_ge(v_made, g + 1)
                fn(vt[:, b % 2, jt, 8 * half:8 * half + 8, 0:DH],
                   bank[:, v_bank(g)].rearrange("p (h d) -> p h d", h=8), ACT.Copy, scale=V_SCALE
                   ).then_inc(vh_made, 1)

            def values_copy(g):
                act.wait_ge(v_made, g + 1)
                if g >= 10:
                    act.wait_ge(vp_made, g - 9)
                fn(vraw[:, g % 2], bank[:, v_bank(g)], ACT.Copy, scale=V_SCALE).then_inc(v_copied, 1)

            values_hi(0)
            values_hi(1)
            latent_gain(0)
            values_hi(2)

            def t_hi(n):
                act.wait_ge(t_made, n + 1)
                if n >= 4:
                    act.wait_ge(s_made, 2 * (n - 3))
                fn(th[:, n % 4], bank[:, TB_B, 0:S], ACT.Copy, scale=SCALE
                   ).then_inc(th_made, 1)
                if n >= 2:
                    if n >= 4:
                        act.wait_ge(tl_made, n - 1)
                    fn(traw[:, n % 2], bank[:, TB_B, 0:S], ACT.Copy, scale=SCALE).then_inc(t_copied, 1)

            t_hi(0)
            values_hi(3)
            t_hi(1)

            def exponent(n, c):
                u = 2 * n + c
                act.wait_ge(max_made, u + 1)
                if n >= 2:
                    act.wait_ge(pT_made, u - 3)
                fn(pr[:, u % 4], bank[:, S_B + c], ACT.Exp, bias=nmax[:, u:u + 1],
                   accum_out=psm[:, u:u + 1]).then_inc(exp_made, 1)

            def probs_hi(n, c):
                act.wait_ge(pT_made, 2 * n + c + 1)
                if n >= 2:
                    act.wait_ge(o_made, n - 1)
                fn(pth[:, n % 2, c].rearrange("p a q -> p (a q)"), bank[:, T_B + c], ACT.Copy,
                   scale=P_SCALE).then_inc(pth_made, 1)

            def pair_copy(j):
                act.wait_ge(oT_made, j + 1)
                if j >= 2:
                    act.wait_ge(y_part, j - 1)
                fn(oT[:, j % 2], bank[:, O_B, P:P + S], ACT.Copy,
                   scale=1.0 / (P_SCALE * V_SCALE)).then_inc(oT_sb, 1)

            def x2T_copy(b):
                act.wait_ge(x2T_made, b + 1)
                fn(xT[:, b], bank[:, V_B, 0:S], ACT.Copy).then_inc(xT_made, 1)

            def gate_exp(i):
                act.wait_ge(top_made, i + 1)
                ks = G_TILES[i]
                fn(ge2[:, ks], top[:, ks, 0:2], ACT.Exp, scale=-1.0).then_inc(ge_made, 1)

            def silu(m, k):
                i = 2 * m + k
                act.wait_ge(gu_made, 4 * m + 2 * k + 1)
                if i >= 2:
                    act.wait_ge(h_made, i - 1)
                fn(sg[:, i % 2], bank[:, GU_B[2 * k]], ACT.Silu).then_inc(sg_made, 1)

            def hidden_hi(m, k):
                act.wait_ge(h_made, 2 * m + k + 1)
                if m < 2:
                    act.wait_ge(o_made, NH - 1 + m)
                else:
                    act.wait_ge(dn_made, m - 1)
                fn(hh[:, m % 2, k], hT[:, k], ACT.Copy).then_inc(hh_made, 1)

            for u in range(2 * STEPS):
                n, c = u // 2, u % 2
                if c == 0 and n % 2 == 1 and n >= 5:
                    pair_copy((n - 5) // 2)
                if 0 <= u - 3 < 2 * NH:
                    probs_hi((u - 3) // 2, (u - 3) % 2)
                if n < NH:
                    exponent(n, c)
                if c == 0 and n + 2 < NH:
                    t_hi(n + 2)
                for g in v_at.get(u, []):
                    values_hi(g) if g < 8 else values_copy(g)
                for b in range(B):
                    if b and u == lat_at(b, "turn"):
                        latent_gain(b)
                    if b < LAST_NORM and u == x2_at(b, "turn"):
                        x2T_copy(b)
                if u == ROUTE_AT + 3:
                    gate_exp(0)
                if u == 2 * NH + 2:
                    silu(0, 0)

            for m in range(2 * E):
                if m == 2:
                    x2T_copy(B - 1)
                if m == 4:
                    gate_exp(1)
                for k in range(1 if m == 0 else 0, FC):
                    silu(m, k)
                for k in range(FC):
                    hidden_hi(m, k)

        @block.gpsimd
        def _(pool):
            pool.wait_ge(d_fr, 16)
            nc.gpsimd.tensor_tensor(fqk[:], fr_sb[:, 0], fr_sb[:, 1], ALU.mult).then_inc(fqk_made, 1)

            rstds = [0]

            def rstd(i, tiles):
                rstds[0] += 1
                pool.wait_ge(ve_made, rstds[0])
                nc.gpsimd.tensor_tensor(rs[:, i, tiles], ve[:, i, tiles],
                                        cst[:, HALF0:HALF0 + 8][:, tiles], ALU.pow).then_inc(rs_made, 1)

            pool.wait_ge(d_cst, 16)
            rstd(0, slice(0, 8))

            def split_context(c):
                pool.wait_ge(kvh_made, c + 1)
                at = (slice(None), slice(None), slice(c * P, c * P + P))
                nc.gpsimd.tensor_tensor(kvl[at], kv[at], kvh[at], ALU.subtract).then_inc(kvl_made, 1)

            pool.wait_ge(wvh_made, 1)
            nc.gpsimd.tensor_tensor(wvl[:], wv_sb[:], wvh[:], ALU.subtract).then_inc(wvl_made, 1)
            for c in range(C):
                split_context(c)
            for i in (1, 2):
                rstd(i, slice(0, 8, B))

            def t_lo(n):
                pool.wait_ge(t_copied, n - 1)
                if n >= 4:
                    pool.wait_ge(s_made, 2 * (n - 3))
                nc.gpsimd.tensor_tensor(tl[:, n % 4], traw[:, n % 2], th[:, n % 4].bitcast(F32),
                                        ALU.subtract).then_inc(tl_made, 1)

            def split_values(g):
                b, jt, half = V_GROUPS[g]
                raw = vraw[:, g % 2].rearrange("p (h d) -> p h d", h=8)
                vh = vt[:, b % 2, jt, 8 * half:8 * half + 8, 0:DH]
                vl = vt[:, b % 2, jt, 8 * half:8 * half + 8, DH:2 * DH]
                pool.wait_ge(v_copied, g - 7)
                if b >= 2:
                    pool.wait_ge(o_made, H * (b - 1))
                nc.gpsimd.tensor_tensor(vh, raw, one.unsqueeze(2).to_broadcast([P, 8, DH]), ALU.mult
                                        ).then_inc(vh_made, 1)
                pool.wait_ge(vh_made, g + 1)
                nc.gpsimd.tensor_tensor(vl, raw, vh, ALU.subtract).then_inc(vp_made, 1)

            for u in range(2 * STEPS):
                n = u // 2
                if u % 2 == 0 and n + 2 < NH:
                    t_lo(n + 2)
                for g in v_at.get(u, []):
                    if g >= 8:
                        split_values(g)
                if 5 <= n < 5 + 2 * E and u % 4 == 3:
                    e = (n - 5) // 2
                    pool.wait_ge(wgh_made, e + 1)
                    nc.gpsimd.tensor_tensor(wgl[:, e], wraw[:, e % 2], wgh[:, e], ALU.subtract
                                            ).then_inc(wgl_made, 1)
                if (u - WD_AT[0]) // 4 in range(4):
                    i, step = (u - WD_AT[0]) // 4, (u - WD_AT[0]) % 4
                    cols = slice(512 * i, 512 * (i + 1))
                    if step == 0:
                        pool.wait_ge(d_wd, 16)
                        nc.gpsimd.tensor_tensor(wd[:, cols], wd[:, cols],
                                                cst[:, WS0:WS0 + 1].to_broadcast([P, 512]), ALU.mult
                                                ).then_inc(wds_made, 1)
                    if step == 1:
                        pool.wait_ge(wds_made, i + 1)
                        nc.gpsimd.tensor_tensor(wdh[:, cols], wd[:, cols],
                                                one.to_broadcast([P, 512]), ALU.mult
                                                ).then_inc(wdh_made, 1)
                    if step == 2:
                        pool.wait_ge(wdh_made, i + 1)
                        nc.gpsimd.tensor_tensor(wdl[:, cols], wd[:, cols], wdh[:, cols], ALU.subtract
                                                ).then_inc(wdl_made, 1)
                for b in range(1, B):
                    if u == lat_at(b, "var"):
                        rstd(1, slice(b, 8, B))
                    if u == lat_at(b, "var2"):
                        rstd(2, slice(b, 8, B))
                for b in range(LAST_NORM):
                    if u == x2_at(b, "var"):
                        rstd(3, slice(b, 8, B))
                    if u == x2_at(b, "split"):
                        pool.wait_ge(xTh_made, b + 1)
                        nc.gpsimd.tensor_tensor(xTl[:, b], xT[:, b], xTh[:, b], ALU.subtract
                                                ).then_inc(xTl_made, 1)
            def hidden_lo(m, k):
                pool.wait_ge(hh_made, 2 * m + k + 1)
                nc.gpsimd.tensor_tensor(hl[:, m % 2, k], hT[:, k], hh[:, m % 2, k], ALU.subtract
                                        ).then_inc((hl0_made, hl1_made)[k], 1)

            b = B - 1
            rstd(3, slice(b, 8, B))
            hidden_lo(0, 0)
            hidden_lo(0, 1)
            pool.wait_ge(xTh_made, b + 1)
            nc.gpsimd.tensor_tensor(xTl[:, b], xT[:, b], xTh[:, b], ALU.subtract).then_inc(xTl_made, 1)
            for m in range(1, 2 * E):
                if m == E + 4:
                    rstd(4, slice(0, 8, B))
                    rstd(4, slice(1, 8, B))
                hidden_lo(m, 0)
                if m < 2 * E - 1:
                    hidden_lo(m, 1)
            for b in (B - 2, B - 1):
                rstd(4, slice(b, 8, B))

        @block.vector
        def _(dve):
            v = nc.vector
            own = [0]

            def mark(ins):
                own[0] += 1
                ins.then_inc(dve_own, 1)

            def settle():
                dve.wait_ge(dve_own, own[0])

            def tile_stats(i, src, tiles):
                for k in tiles:
                    mark(v.bn_stats(st[:, i, k], src[:, k // B, k % B]))

            def variances(i, tiles):
                settle()
                for k in tiles:
                    mark(v.bn_aggr(mv[:, i, k], st[:, i, k]))
                settle()
                ks = slice(tiles[0], 8, tiles[1] - tiles[0])
                v.tensor_scalar(ve[:, i, ks], mv[:, i, ks, 1], EPS, None, ALU.add).then_inc(ve_made, 1)

            def statistics(i, src, tiles):
                tile_stats(i, src, tiles)
                variances(i, tiles)

            rstds = [0]

            def await_rstd():
                rstds[0] += 1
                dve.wait_ge(rs_made, rstds[0])

            def centre(i, dst, src, k):
                return v.tensor_scalar(dst[:, k // B, k % B], src[:, k // B, k % B], mv[:, i, k, 0:1],
                                       rs[:, i, k:k + 1], ALU.subtract, ALU.mult)

            every = list(range(8))
            dve.wait_ge(d_ctx, 32)
            statistics(0, ct, every)
            await_rstd()
            for k in every[:B]:
                last = centre(0, ct, ct, k)
            last.then_inc(zc_made, 1)
            both = [P, 2 * B, M]
            dve.wait_ge(qkv_made, 1)
            dve.wait_ge(fqk_made, 1)
            mark(v.tensor_tensor(qw, bank[:, 1].rearrange("p (a m) -> p a m", m=M),
                                 fqk[:].unsqueeze(1).to_broadcast(both), ALU.mult))
            dve.wait_ge(qkv_made, 2)
            settle()
            v.tensor_tensor(qk, bank[:, 2].rearrange("p (a m) -> p a m", m=M), qw, ALU.mult
                            ).then_inc(qk_sb, 1)
            for k in every[B:]:
                last = centre(0, ct, ct, k)
            last.then_inc(zc_made, 1)
            dve.wait_ge(fs_made, 1)
            v.tensor_reduce(fnmax[:, 0:1], bank[0:B * FH, 0, 0:M], AX_X, ALU.max, negate=True
                            ).then_inc(fnmax_made, 1)
            dve.wait_ge(qkv_made, 3)
            dve.wait_ge(d_fr, 16)
            mark(v.tensor_tensor(vw.rearrange("p b a m -> p (b a) m"),
                                 bank[:, 3].rearrange("p (a m) -> p a m", m=M),
                                 fr_sb[:, 2].unsqueeze(1).to_broadcast(both), ALU.mult))

            def fold_lo(g):
                dve.wait_ge(ah_made, g + 1)
                v.tensor_tensor(al[:, 4 * g:4 * g + 4].rearrange("p h d -> p (h d)"), bank[:, 4 + g % 2],
                                ah[:, 4 * g:4 * g + 4].rearrange("p h d -> p (h d)"), ALU.subtract
                                ).then_inc(al_made, 1)

            dve.wait_ge(fexp_made, 1)
            mark(v.reciprocal(frcp[:, 0:1], fsum[:, 0:1]))
            settle()
            v.tensor_scalar(fattn[:], fexp[:], frcp[:, 0:1], None, ALU.mult).then_inc(fattn_sb, 1)
            dve.wait_ge(fab_made, 1)
            v.tensor_tensor(ot, vw,
                            bank[:, 0, 256:512].rearrange("p (b m) -> p b m", b=B).unsqueeze(2)
                            .to_broadcast([P, B, 2, M]), ALU.mult).then_inc(ot_sb, 1)
            fold_lo(0)
            fold_lo(1)
            for c in range(C):
                dve.wait_ge(kv_made, c + 1)
                v.tensor_copy(kvh[:, :, c * P:(c + 1) * P], kv[:, :, c * P:(c + 1) * P]
                              ).then_inc(kvh_made, 1)

            def split_latents(b):
                dve.wait_ge(kv_made, C + b + 1)
                v.tensor_copy(kvh[:, b, S:J], kv[:, b, S:J]).then_inc(kvh_made, 1)
                dve.wait_ge(kvh_made, C + b + 1)
                v.tensor_tensor(kvl[:, b, S:J], kv[:, b, S:J], kvh[:, b, S:J], ALU.subtract
                                ).then_inc(kvl_made, 1)

            def values_lo(g):
                b, jt, half = V_GROUPS[g]
                dve.wait_ge(vh_made, g + 1)
                heads = slice(8 * half, 8 * half + 8)
                v.scalar_tensor_tensor(out=vt[:, b % 2, jt, heads, DH:2 * DH],
                                       in0=bank[:, v_bank(g)].rearrange("p (h d) -> p h d", h=8),
                                       scalar=V_SCALE, in1=vt[:, b % 2, jt, heads, 0:DH],
                                       op0=ALU.mult, op1=ALU.subtract).then_inc(vl_made, 1)

            def first_norm_out(b):
                await_rstd()
                for k in (b, B + b):
                    mark(centre(1, x1, xt, k))

            def latents_out(b):
                await_rstd()
                for k in (b, B + b):
                    last = centre(2, zl, x1, k)
                last.then_inc(zl_made, 1)

            def t_lo(n):
                dve.wait_ge(th_made, n + 1)
                v.scalar_tensor_tensor(out=tl[:, n % 4], in0=bank[:, TB_B, 0:S],
                                       scalar=SCALE, in1=th[:, n % 4].bitcast(F32), op0=ALU.mult,
                                       op1=ALU.subtract).then_inc(tl_made, 1)

            def add_rest(c):
                dve.wait_ge(y1_made, c + 2)
                mark(v.tensor_tensor(xt[:, c, 1:].rearrange("p b d -> p (b d)"),
                                     bank[:, (3, 1)[c], D:B * D],
                                     xt[:, c, 1:].rearrange("p b d -> p (b d)"), ALU.add))

            dve.wait_ge(y1_made, 1)
            mark(v.tensor_tensor(xt[:, :, 0], bank[:, 2, 0:C * D].rearrange("p (c d) -> p c d", c=C),
                                 xt[:, :, 0], ALU.add))
            settle()
            statistics(1, xt, [0, B])
            add_rest(0)
            first_norm_out(0)
            settle()
            statistics(2, x1, [0, B])
            add_rest(1)
            latents_out(0)
            fold_lo(2)
            fold_lo(3)
            values_lo(0)
            split_latents(0)
            values_lo(1)
            t_lo(0)
            values_lo(2)
            t_lo(1)
            values_lo(3)

            def row_max(n, c):
                u = 2 * n + c
                dve.wait_ge(s_made, u + 1)
                v.tensor_reduce(nmax[:, u:u + 1], bank[:, S_B + c], AX_X, ALU.max, negate=True
                                ).then_inc(max_made, 1)

            def sum_reciprocal(n):
                dve.wait_ge(exp_made, 2 * n + 2)
                v.reciprocal(rcp[:, 2 * n:2 * n + 2], psm[:, 2 * n:2 * n + 2]).then_inc(rcp_made, 1)

            def normalise(n):
                dve.wait_ge(rcp_made, n + 1)
                dve.wait_ge(o_made, n + 1)
                if n >= 2:
                    dve.wait_ge(oT_sb, n // 2 if n % 2 == 0 else (n - 1) // 2)
                v.tensor_tensor(on[:, n // 2 % 2, :, n % 2],
                                bank[:, O_B, 0:C * DH].rearrange("p (c d) -> p c d", c=C),
                                rcp[:, 2 * n:2 * n + 2].unsqueeze(2).to_broadcast([P, C, DH]), ALU.mult
                                ).then_inc(o_sb, 1)

            def probs_lo(n, c):
                dve.wait_ge(pth_made, 2 * n + c + 1)
                v.scalar_tensor_tensor(out=ptl[:, n % 2, c].rearrange("p a q -> p (a q)"),
                                       in0=bank[:, T_B + c], scalar=P_SCALE,
                                       in1=pth[:, n % 2, c].rearrange("p a q -> p (a q)"),
                                       op0=ALU.mult, op1=ALU.subtract).then_inc(ptl_made, 1)

            def second_norm_in(b):
                dve.wait_ge(y_part, H // 2 * (b + 1))
                ins = v.tensor_tensor(acc[:, :, b], bank[:, Y_B, 0:C * D].rearrange(
                    "p (c d) -> p c d", c=C), x1[:, :, b], ALU.add)
                ins.then_inc(y_used, 1)

            def second_norm_out(b):
                await_rstd()
                for c in range(C):
                    last = centre(3, x2, acc, c * B + b)
                last.then_inc(x2_made, 1)

            def split_x2T(b):
                dve.wait_ge(xT_made, b + 1)
                v.tensor_copy(xTh[:, b], xT[:, b]).then_inc(xTh_made, 1)

            def hidden(m, k):
                i = 2 * m + k
                dve.wait_ge(sg_made, i + 1)
                dve.wait_ge(gu_made, 4 * m + 2 * k + 2)
                if m >= 1:
                    dve.wait_ge(*((hl0_made, m) if k == 0 else (hl1_made, m)))
                v.scalar_tensor_tensor(out=hT[:, k], in0=bank[:, GU_B[2 * k + 1]], scalar=H_SCALE,
                                       in1=sg[:, i % 2], op0=ALU.mult, op1=ALU.mult
                                       ).then_inc(h_made, 1)

            def hidden_lo(m):
                dve.wait_ge(hh_made, 2 * m + 2)
                v.tensor_tensor(hl[:, m % 2, 1], hT[:, 1], hh[:, m % 2, 1], ALU.subtract
                                ).then_inc(hl1_made, 1)

            def largest(i):
                ks = G_TILES[i]
                dve.wait_ge(lg_made, i + 1)
                v.tensor_copy(lg[:, ks], bank[:, V_B, ks.start * E:ks.stop * E].rearrange(
                    "p (k e) -> p k e", e=E)).then_inc(lg_copied, 1)
                dve.wait_ge(lg_copied, i + 1)
                for k in range(ks.start, ks.stop):
                    mark(v.max(top[:, k], lg[:, k]))

            def their_experts(i):
                ks = G_TILES[i]
                settle()
                for k in range(ks.start, ks.stop):
                    mark(v.max_index(topi[:, k], top[:, k], lg[:, k]))
                settle()
                v.tensor_copy(topf[:, ks], topi[:, ks]).then_inc(top_made, 1)

            def sigmoids(i):
                ks = G_TILES[i]
                wide = [P, ks.stop - ks.start, E]
                iota = cst[:, IO0:IO0 + 64].rearrange("p (k e) -> p k e", e=E)[:, ks]
                dve.wait_ge(top_made, i + 1)
                mark(v.tensor_tensor(m0[:, ks], iota, topf[:, ks, 0:1].to_broadcast(wide), ALU.is_equal))
                mark(v.tensor_tensor(m1[:, ks], iota, topf[:, ks, 1:2].to_broadcast(wide), ALU.is_equal))
                dve.wait_ge(ge_made, i + 1)
                mark(v.tensor_scalar(gn[:, ks], ge2[:, ks], 1.0, None, ALU.add))
                settle()
                mark(v.reciprocal(ge2[:, ks], gn[:, ks]))

            def reciprocal_of_sum(i):
                ks = G_TILES[i]
                settle()
                mark(v.tensor_tensor(gs[:, ks], ge2[:, ks, 0], ge2[:, ks, 1], ALU.add))
                settle()
                mark(v.tensor_scalar(gs[:, ks], gs[:, ks], 1e-10, H_SCALE * W_SCALE, ALU.add, ALU.mult))
                settle()
                mark(v.reciprocal(gr[:, ks], gs[:, ks]))

            def spread_gates(i):
                ks = G_TILES[i]
                wide = [P, ks.stop - ks.start, E]
                settle()
                mark(v.tensor_tensor(gn[:, ks], ge2[:, ks],
                                     gr[:, ks].unsqueeze(2).to_broadcast([P, wide[1], 2]), ALU.mult))
                settle()
                mark(v.tensor_tensor(m0[:, ks], m0[:, ks], gn[:, ks, 0:1].to_broadcast(wide), ALU.mult))
                mark(v.tensor_tensor(m1[:, ks], m1[:, ks], gn[:, ks, 1:2].to_broadcast(wide), ALU.mult))
                settle()
                mark(v.tensor_tensor(gate[:, ks], m0[:, ks], m1[:, ks], ALU.add))

            for u in range(2 * STEPS):
                n, c = u // 2, u % 2
                if c == 0 and 3 <= n < NH + 3:
                    normalise(n - 3)
                if n < NH:
                    row_max(n, c)
                if 0 <= u - 3 < 2 * NH:
                    probs_lo((u - 3) // 2, (u - 3) % 2)
                if c == 1 and 1 <= n <= NH:
                    sum_reciprocal(n - 1)
                for g in v_at.get(u - 1, []):
                    if g < 8:
                        values_lo(g)
                if 4 <= n < 4 + 2 * E and n % 2 == 0 and c == 0:
                    e = (n - 4) // 2
                    dve.wait_ge(d_raw[e % 2], 16 * (e // 2 + 1))
                    v.tensor_copy(wgh[:, e], wraw[:, e % 2]).then_inc(wgh_made, 1)
                for b in range(1, B):
                    mine = [b, B + b]
                    if u == lat_at(b, "stats"):
                        tile_stats(1, xt, mine)
                    if u == lat_at(b, "var"):
                        variances(1, mine)
                    if u == lat_at(b, "norm1"):
                        first_norm_out(b)
                    if u == lat_at(b, "stats2"):
                        settle()
                        tile_stats(2, x1, mine)
                    if u == lat_at(b, "var2"):
                        variances(2, mine)
                    if u == lat_at(b, "norm2"):
                        latents_out(b)
                    if u == lat_at(b, "split"):
                        split_latents(b)
                for b in range(LAST_NORM):
                    mine = [b, B + b]
                    if u == x2_at(b, "add"):
                        second_norm_in(b)
                    if u == x2_at(b, "stats"):
                        dve.wait_ge(y_used, b + 1)
                        tile_stats(3, acc, mine)
                    if u == x2_at(b, "var"):
                        variances(3, mine)
                    if u == x2_at(b, "norm"):
                        second_norm_out(b)
                    if u == x2_at(b, "split"):
                        split_x2T(b)
                for i, piece in enumerate((largest, their_experts, None, None, sigmoids,
                                           reciprocal_of_sum, spread_gates)):
                    if piece and u == ROUTE_AT + 1 + i:
                        piece(0)
                if u == 2 * NH + 4:
                    hidden(0, 0)
            def add_tiles(m, at, ts):
                hf, e = m // E, m % E
                for t in ts:
                    b, c = 2 * hf + t // C, t % C
                    last = v.scalar_tensor_tensor(out=acc[:, c, b], in0=bank[:, at, t * D:(t + 1) * D],
                                                  scalar=gate[:, C * b + c, e:e + 1],
                                                  in1=(x2 if e == 0 else acc)[:, c, b],
                                                  op0=ALU.mult, op1=ALU.add)
                    if t < ts[-1]:
                        mark(last)
                return last

            def accumulate(m):
                dve.wait_ge(dn_made, m + 1)
                settle()
                add_tiles(m, DN_B[m % 2], range(4)).then_inc(dn_used, 1)
                dve.wait_ge(dn_used, m + 1)

            def final_centre(tiles):
                await_rstd()
                for k in tiles:
                    centre(4, acc, acc, k).then_inc(fin_made, 1)

            hidden(0, 1)
            second_norm_in(B - 1)
            dve.wait_ge(y_used, B)
            statistics(3, acc, [B - 1, 2 * B - 1])
            second_norm_out(B - 1)
            hidden(1, 0)
            hidden(1, 1)
            split_x2T(B - 1)
            largest(1)
            their_experts(1)
            batch = [[b, B + b] for b in range(B)]
            for m in range(1, 2 * E - 1):
                if m > 1:
                    hidden(m, 0)
                    hidden(m, 1)
                if m < 2 * E - 2:
                    accumulate(m - 1)
                if m == 3:
                    sigmoids(1)
                if m == 4:
                    reciprocal_of_sum(1)
                if m == 5:
                    spread_gates(1)
                if m == E + 1:
                    tile_stats(4, acc, batch[0])
                if m == E + 2:
                    tile_stats(4, acc, batch[1])
                if m == E + 3:
                    variances(4, batch[0])
                    variances(4, batch[1])
                if m == E + 4:
                    final_centre(batch[0])
                if m == E + 5:
                    final_centre(batch[1])
            hidden(2 * E - 1, 0)
            hidden(2 * E - 1, 1)
            accumulate(2 * E - 3)
            hidden_lo(2 * E - 1)
            accumulate(2 * E - 2)
            for i in range(2):
                dve.wait_ge(dn_made, 2 * E + i)
                mark(add_tiles(2 * E - 1, GU_B[i], range(2 * i, 2 * i + 2)))
                settle()
                statistics(4, acc, batch[2 + i])
                if i == 1:
                    final_centre(batch[2])
            final_centre(batch[3])


def constants():
    import numpy as np
    k = np.zeros((P, NCONST), np.float32)
    s, f = np.arange(S)[:, None], np.arange(M)[None, :]
    angle = 2 * np.pi * ((s * f) % S) / S
    cs = np.concatenate([np.cos(angle), np.sin(angle)], 1).astype(np.float32)
    for c in range(C):
        k[:, CS0 + c * P:CS0 + (c + 1) * P] = cs[c * P:(c + 1) * P]
    k[:, CST0:CST0 + S] = cs.T
    k[:, ID0:ID0 + P] = np.eye(P)
    for p in range(P):
        k[p, EB0 + 48 + p // HD] = 1
        for b in range(B):
            k[16 * b + p // HD, SEL0 + b * P + p] = 1
    k[:, IO0:IO0 + 64] = np.tile(np.arange(E), 8)
    k[:, HALF0:HALF0 + 8] = -0.5
    k[:, LEN0:LEN0 + B] = S
    k[:, WS0] = W_SCALE
    return k


def kernel(**inputs):
    import numpy as np
    import concourse.bacc as bacc
    from concourse.bass_utils import run_bass_kernel_spmd

    a = {n: np.asarray(v) for n, v in inputs.items()}
    inner = H * DH
    wkv = a["L0_xattn_Wkv"]
    arrays = {
        "x": a["x"],
        "ctx_in": a["ctx_1024"],
        "w_qkvT": a["L0_attn_w_qkv"].T,
        "b_qkv": a["L0_attn_b_qkv"][None],
        "w_outT": a["L0_attn_w_out"].T,
        "b_out": a["L0_attn_b_out"][None],
        "freqT": np.concatenate([a[f"L0_attn_freq_{n}"].transpose(0, 2, 1).reshape(D, M) for n in "qkv"], 1),
        "ln_par": np.stack([a[f"L0_xattn_ln_{n}"] for n in ("m_g", "m_b", "l_g", "l_b")], 1),
        "wqT": a["L0_xattn_Wq"].T,
        "wkT": wkv[:, :inner].T,
        "wv": wkv[:, inner:],
        "wout": a["L0_xattn_Wout"],
        "routerT": a["L0_ffn_router_w"].T,
        "w_gu": np.concatenate([a["L0_ffn_w_gate"], a["L0_ffn_w_up"]], 2).transpose(1, 0, 2),
        "w_down": a["L0_ffn_w_down"],
        "consts": constants(),
    }
    arrays = {n: np.ascontiguousarray(v) for n, v in arrays.items()}
    nc = bacc.Bacc("TRN2", target_bir_lowering=False, num_devices=1)
    args = [nc.dram_tensor(f"in_{n}", v.shape, mybir.dt.from_np(v.dtype), kind="ExternalInput").ap()
            for n, v in arrays.items()]
    out = nc.dram_tensor("out", (B, S, D), F32, kind="ExternalOutput").ap()
    decoder_layer(nc, *args, out)
    r = run_bass_kernel_spmd(nc, [{f"in_{n}": v for n, v in arrays.items()}], core_ids=[0])
    return r.results[0]["out"]
```
